# Optimizing a Trainium2 kernel written in Bass

```python
import numpy as np
import jax
import jax.numpy as jnp

def _softmax(x, axis=-1):
    return jax.nn.softmax(x, axis=axis)

def _gelu(x):
    return jax.nn.gelu(x, approximate=True)

def _silu(x):
    return jax.nn.silu(x)

def _sigmoid(x):
    return jax.nn.sigmoid(x)

def _layernorm(x, axis=-1, eps=1e-05):
    m = jnp.mean(x, axis=axis, keepdims=True)
    v = jnp.var(x, axis=axis, keepdims=True)
    return (x - m) / jnp.sqrt(v + eps)

def _scatter_add(tgt, idx, src, axis=0):
    return tgt.at[idx].add(src)

def _segment_sum(src, seg, n):
    return jax.ops.segment_sum(src, seg, n)
kernel_name = 'mk_rec_standalone_d1_rec_r8_054f4d'

def setup_inputs(seed: int=0):
    np.random.seed(seed)
    _w = jnp.asarray

    def _rec_inputs():
        import jax
        import jax.numpy as jnp
        _rk = jax.random.key(seed)
        r_sequence_ids = jnp.stack([jax.random.randint(jax.random.fold_in(jax.random.fold_in(_rk, 1), 0), (1024,), 5, 99326, jnp.int32), jax.random.randint(jax.random.fold_in(jax.random.fold_in(_rk, 1), 1), (1024,), 220, 99995, jnp.int32), jax.random.randint(jax.random.fold_in(jax.random.fold_in(_rk, 1), 2), (1024,), 265, 99940, jnp.int32), jax.random.randint(jax.random.fold_in(jax.random.fold_in(_rk, 1), 3), (1024,), 402, 99940, jnp.int32), jax.random.randint(jax.random.fold_in(jax.random.fold_in(_rk, 1), 4), (1024,), 225, 99931, jnp.int32), jax.random.randint(jax.random.fold_in(jax.random.fold_in(_rk, 1), 5), (1024,), 106, 12497, jnp.int32), jax.random.randint(jax.random.fold_in(jax.random.fold_in(_rk, 1), 6), (1024,), 132, 99942, jnp.int32), jax.random.randint(jax.random.fold_in(jax.random.fold_in(_rk, 1), 7), (1024,), 167, 12486, jnp.int32), jax.random.randint(jax.random.fold_in(jax.random.fold_in(_rk, 1), 8), (1024,), 58, 99725, jnp.int32), jax.random.randint(jax.random.fold_in(jax.random.fold_in(_rk, 1), 9), (1024,), 63, 99973, jnp.int32), jax.random.randint(jax.random.fold_in(jax.random.fold_in(_rk, 1), 10), (1024,), 38, 99849, jnp.int32), jax.random.randint(jax.random.fold_in(jax.random.fold_in(_rk, 1), 11), (1024,), 123, 99892, jnp.int32), jax.random.randint(jax.random.fold_in(jax.random.fold_in(_rk, 1), 12), (1024,), 56, 99898, jnp.int32), jax.random.randint(jax.random.fold_in(jax.random.fold_in(_rk, 1), 13), (1024,), 37, 99812, jnp.int32), jax.random.randint(jax.random.fold_in(jax.random.fold_in(_rk, 1), 14), (1024,), 27, 12482, jnp.int32), jax.random.randint(jax.random.fold_in(jax.random.fold_in(_rk, 1), 15), (1024,), 0, 99865, jnp.int32), jax.random.randint(jax.random.fold_in(jax.random.fold_in(_rk, 1), 16), (1024,), 56, 99762, jnp.int32), jax.random.randint(jax.random.fold_in(jax.random.fold_in(_rk, 1), 17), (1024,), 405, 99982, jnp.int32), jax.random.randint(jax.random.fold_in(jax.random.fold_in(_rk, 1), 18), (1024,), 30, 99955, jnp.int32), jax.random.randint(jax.random.fold_in(jax.random.fold_in(_rk, 1), 19), (1024,), 40, 99908, jnp.int32), jax.random.randint(jax.random.fold_in(jax.random.fold_in(_rk, 1), 20), (1024,), 58, 12490, jnp.int32), jax.random.randint(jax.random.fold_in(jax.random.fold_in(_rk, 1), 21), (1024,), 5, 99876, jnp.int32), jax.random.randint(jax.random.fold_in(jax.random.fold_in(_rk, 1), 22), (1024,), 117, 99957, jnp.int32), jax.random.randint(jax.random.fold_in(jax.random.fold_in(_rk, 1), 23), (1024,), 172, 99956, jnp.int32), jax.random.randint(jax.random.fold_in(jax.random.fold_in(_rk, 1), 24), (1024,), 331, 99903, jnp.int32), jax.random.randint(jax.random.fold_in(jax.random.fold_in(_rk, 1), 25), (1024,), 10, 99683, jnp.int32), jax.random.randint(jax.random.fold_in(jax.random.fold_in(_rk, 1), 26), (1024,), 38, 99669, jnp.int32), jax.random.randint(jax.random.fold_in(jax.random.fold_in(_rk, 1), 27), (1024,), 376, 99905, jnp.int32), jax.random.randint(jax.random.fold_in(jax.random.fold_in(_rk, 1), 28), (1024,), 105, 12487, jnp.int32), jax.random.randint(jax.random.fold_in(jax.random.fold_in(_rk, 1), 29), (1024,), 39, 99994, jnp.int32), jax.random.randint(jax.random.fold_in(jax.random.fold_in(_rk, 1), 30), (1024,), 38, 99982, jnp.int32), jax.random.randint(jax.random.fold_in(jax.random.fold_in(_rk, 1), 31), (1024,), 3, 99946, jnp.int32), jax.random.randint(jax.random.fold_in(jax.random.fold_in(_rk, 1), 32), (1024,), 79, 99983, jnp.int32), jax.random.randint(jax.random.fold_in(jax.random.fold_in(_rk, 1), 33), (1024,), 7, 99947, jnp.int32), jax.random.randint(jax.random.fold_in(jax.random.fold_in(_rk, 1), 34), (1024,), 67, 99937, jnp.int32), jax.random.randint(jax.random.fold_in(jax.random.fold_in(_rk, 1), 35), (1024,), 90, 99989, jnp.int32), jax.random.randint(jax.random.fold_in(jax.random.fold_in(_rk, 1), 36), (1024,), 6, 99980, jnp.int32), jax.random.randint(jax.random.fold_in(jax.random.fold_in(_rk, 1), 37), (1024,), 71, 99917, jnp.int32), jax.random.randint(jax.random.fold_in(jax.random.fold_in(_rk, 1), 38), (1024,), 44, 99770, jnp.int32), jax.random.randint(jax.random.fold_in(jax.random.fold_in(_rk, 1), 39), (1024,), 23, 99988, jnp.int32), jax.random.randint(jax.random.fold_in(jax.random.fold_in(_rk, 1), 40), (1024,), 48, 99913, jnp.int32), jax.random.randint(jax.random.fold_in(jax.random.fold_in(_rk, 1), 41), (1024,), 45, 99942, jnp.int32), jax.random.randint(jax.random.fold_in(jax.random.fold_in(_rk, 1), 42), (1024,), 130, 99942, jnp.int32), jax.random.randint(jax.random.fold_in(jax.random.fold_in(_rk, 1), 43), (1024,), 26, 99979, jnp.int32), jax.random.randint(jax.random.fold_in(jax.random.fold_in(_rk, 1), 44), (1024,), 62, 99914, jnp.int32), jax.random.randint(jax.random.fold_in(jax.random.fold_in(_rk, 1), 45), (1024,), 246, 12498, jnp.int32), jax.random.randint(jax.random.fold_in(jax.random.fold_in(_rk, 1), 46), (1024,), 139, 99810, jnp.int32), jax.random.randint(jax.random.fold_in(jax.random.fold_in(_rk, 1), 47), (1024,), 129, 99751, jnp.int32), jax.random.randint(jax.random.fold_in(jax.random.fold_in(_rk, 1), 48), (1024,), 176, 99915, jnp.int32), jax.random.randint(jax.random.fold_in(jax.random.fold_in(_rk, 1), 49), (1024,), 111, 99945, jnp.int32), jax.random.randint(jax.random.fold_in(jax.random.fold_in(_rk, 1), 50), (1024,), 224, 99916, jnp.int32), jax.random.randint(jax.random.fold_in(jax.random.fold_in(_rk, 1), 51), (1024,), 89, 99895, jnp.int32), jax.random.randint(jax.random.fold_in(jax.random.fold_in(_rk, 1), 52), (1024,), 347, 99926, jnp.int32), jax.random.randint(jax.random.fold_in(jax.random.fold_in(_rk, 1), 53), (1024,), 33, 99963, jnp.int32), jax.random.randint(jax.random.fold_in(jax.random.fold_in(_rk, 1), 54), (1024,), 9, 99964, jnp.int32), jax.random.randint(jax.random.fold_in(jax.random.fold_in(_rk, 1), 55), (1024,), 61, 99812, jnp.int32), jax.random.randint(jax.random.fold_in(jax.random.fold_in(_rk, 1), 56), (1024,), 88, 99907, jnp.int32), jax.random.randint(jax.random.fold_in(jax.random.fold_in(_rk, 1), 57), (1024,), 84, 99981, jnp.int32), jax.random.randint(jax.random.fold_in(jax.random.fold_in(_rk, 1), 58), (1024,), 356, 99987, jnp.int32), jax.random.randint(jax.random.fold_in(jax.random.fold_in(_rk, 1), 59), (1024,), 14, 99914, jnp.int32), jax.random.randint(jax.random.fold_in(jax.random.fold_in(_rk, 1), 60), (1024,), 24, 99983, jnp.int32), jax.random.randint(jax.random.fold_in(jax.random.fold_in(_rk, 1), 61), (1024,), 63, 99972, jnp.int32), jax.random.randint(jax.random.fold_in(jax.random.fold_in(_rk, 1), 62), (1024,), 257, 99965, jnp.int32), jax.random.randint(jax.random.fold_in(jax.random.fold_in(_rk, 1), 63), (1024,), 14, 99926, jnp.int32), jax.random.randint(jax.random.fold_in(jax.random.fold_in(_rk, 1), 64), (1024,), 200, 99972, jnp.int32), jax.random.randint(jax.random.fold_in(jax.random.fold_in(_rk, 1), 65), (1024,), 176, 99982, jnp.int32), jax.random.randint(jax.random.fold_in(jax.random.fold_in(_rk, 1), 66), (1024,), 26, 99995, jnp.int32), jax.random.randint(jax.random.fold_in(jax.random.fold_in(_rk, 1), 67), (1024,), 41, 99929, jnp.int32), jax.random.randint(jax.random.fold_in(jax.random.fold_in(_rk, 1), 68), (1024,), 17, 99966, jnp.int32), jax.random.randint(jax.random.fold_in(jax.random.fold_in(_rk, 1), 69), (1024,), 60, 99726, jnp.int32), jax.random.randint(jax.random.fold_in(jax.random.fold_in(_rk, 1), 70), (1024,), 15, 99564, jnp.int32), jax.random.randint(jax.random.fold_in(jax.random.fold_in(_rk, 1), 71), (1024,), 21, 99913, jnp.int32), jax.random.randint(jax.random.fold_in(jax.random.fold_in(_rk, 1), 72), (1024,), 82, 12496, jnp.int32), jax.random.randint(jax.random.fold_in(jax.random.fold_in(_rk, 1), 73), (1024,), 161, 99945, jnp.int32), jax.random.randint(jax.random.fold_in(jax.random.fold_in(_rk, 1), 74), (1024,), 180, 99761, jnp.int32), jax.random.randint(jax.random.fold_in(jax.random.fold_in(_rk, 1), 75), (1024,), 78, 99910, jnp.int32), jax.random.randint(jax.random.fold_in(jax.random.fold_in(_rk, 1), 76), (1024,), 34, 99999, jnp.int32), jax.random.randint(jax.random.fold_in(jax.random.fold_in(_rk, 1), 77), (1024,), 15, 99962, jnp.int32), jax.random.randint(jax.random.fold_in(jax.random.fold_in(_rk, 1), 78), (1024,), 142, 99878, jnp.int32), jax.random.randint(jax.random.fold_in(jax.random.fold_in(_rk, 1), 79), (1024,), 127, 99921, jnp.int32), jax.random.randint(jax.random.fold_in(jax.random.fold_in(_rk, 1), 80), (1024,), 41, 12487, jnp.int32), jax.random.randint(jax.random.fold_in(jax.random.fold_in(_rk, 1), 81), (1024,), 121, 99940, jnp.int32), jax.random.randint(jax.random.fold_in(jax.random.fold_in(_rk, 1), 82), (1024,), 10, 99969, jnp.int32), jax.random.randint(jax.random.fold_in(jax.random.fold_in(_rk, 1), 83), (1024,), 93, 99985, jnp.int32), jax.random.randint(jax.random.fold_in(jax.random.fold_in(_rk, 1), 84), (1024,), 54, 12481, jnp.int32), jax.random.randint(jax.random.fold_in(jax.random.fold_in(_rk, 1), 85), (1024,), 2, 99973, jnp.int32), jax.random.randint(jax.random.fold_in(jax.random.fold_in(_rk, 1), 86), (1024,), 1, 99947, jnp.int32), jax.random.randint(jax.random.fold_in(jax.random.fold_in(_rk, 1), 87), (1024,), 12, 99695, jnp.int32), jax.random.randint(jax.random.fold_in(jax.random.fold_in(_rk, 1), 88), (1024,), 136, 99797, jnp.int32), jax.random.randint(jax.random.fold_in(jax.random.fold_in(_rk, 1), 89), (1024,), 219, 99866, jnp.int32), jax.random.randint(jax.random.fold_in(jax.random.fold_in(_rk, 1), 90), (1024,), 6, 99770, jnp.int32), jax.random.randint(jax.random.fold_in(jax.random.fold_in(_rk, 1), 91), (1024,), 100, 99969, jnp.int32), jax.random.randint(jax.random.fold_in(jax.random.fold_in(_rk, 1), 92), (1024,), 126, 99962, jnp.int32), jax.random.randint(jax.random.fold_in(jax.random.fold_in(_rk, 1), 93), (1024,), 29, 99777, jnp.int32), jax.random.randint(jax.random.fold_in(jax.random.fold_in(_rk, 1), 94), (1024,), 50, 99921, jnp.int32), jax.random.randint(jax.random.fold_in(jax.random.fold_in(_rk, 1), 95), (1024,), 141, 99959, jnp.int32), jax.random.randint(jax.random.fold_in(jax.random.fold_in(_rk, 1), 96), (1024,), 0, 99970, jnp.int32), jax.random.randint(jax.random.fold_in(jax.random.fold_in(_rk, 1), 97), (1024,), 76, 99749, jnp.int32), jax.random.randint(jax.random.fold_in(jax.random.fold_in(_rk, 1), 98), (1024,), 130, 99981, jnp.int32), jax.random.randint(jax.random.fold_in(jax.random.fold_in(_rk, 1), 99), (1024,), 334, 12488, jnp.int32), jax.random.randint(jax.random.fold_in(jax.random.fold_in(_rk, 1), 100), (1024,), 230, 99892, jnp.int32), jax.random.randint(jax.random.fold_in(jax.random.fold_in(_rk, 1), 101), (1024,), 118, 99963, jnp.int32), jax.random.randint(jax.random.fold_in(jax.random.fold_in(_rk, 1), 102), (1024,), 144, 99875, jnp.int32), jax.random.randint(jax.random.fold_in(jax.random.fold_in(_rk, 1), 103), (1024,), 134, 99943, jnp.int32), jax.random.randint(jax.random.fold_in(jax.random.fold_in(_rk, 1), 104), (1024,), 28, 99963, jnp.int32), jax.random.randint(jax.random.fold_in(jax.random.fold_in(_rk, 1), 105), (1024,), 2, 99743, jnp.int32), jax.random.randint(jax.random.fold_in(jax.random.fold_in(_rk, 1), 106), (1024,), 43, 12496, jnp.int32), jax.random.randint(jax.random.fold_in(jax.random.fold_in(_rk, 1), 107), (1024,), 10, 99919, jnp.int32), jax.random.randint(jax.random.fold_in(jax.random.fold_in(_rk, 1), 108), (1024,), 100, 99874, jnp.int32), jax.random.randint(jax.random.fold_in(jax.random.fold_in(_rk, 1), 109), (1024,), 227, 99951, jnp.int32), jax.random.randint(jax.random.fold_in(jax.random.fold_in(_rk, 1), 110), (1024,), 3, 99893, jnp.int32), jax.random.randint(jax.random.fold_in(jax.random.fold_in(_rk, 1), 111), (1024,), 10, 99999, jnp.int32), jax.random.randint(jax.random.fold_in(jax.random.fold_in(_rk, 1), 112), (1024,), 96, 99961, jnp.int32), jax.random.randint(jax.random.fold_in(jax.random.fold_in(_rk, 1), 113), (1024,), 31, 99951, jnp.int32), jax.random.randint(jax.random.fold_in(jax.random.fold_in(_rk, 1), 114), (1024,), 271, 99734, jnp.int32), jax.random.randint(jax.random.fold_in(jax.random.fold_in(_rk, 1), 115), (1024,), 14, 99881, jnp.int32), jax.random.randint(jax.random.fold_in(jax.random.fold_in(_rk, 1), 116), (1024,), 57, 99982, jnp.int32), jax.random.randint(jax.random.fold_in(jax.random.fold_in(_rk, 1), 117), (1024,), 49, 12497, jnp.int32), jax.random.randint(jax.random.fold_in(jax.random.fold_in(_rk, 1), 118), (1024,), 6, 99995, jnp.int32), jax.random.randint(jax.random.fold_in(jax.random.fold_in(_rk, 1), 119), (1024,), 65, 99870, jnp.int32), jax.random.randint(jax.random.fold_in(jax.random.fold_in(_rk, 1), 120), (1024,), 29, 12495, jnp.int32), jax.random.randint(jax.random.fold_in(jax.random.fold_in(_rk, 1), 121), (1024,), 9, 99951, jnp.int32), jax.random.randint(jax.random.fold_in(jax.random.fold_in(_rk, 1), 122), (1024,), 47, 99740, jnp.int32), jax.random.randint(jax.random.fold_in(jax.random.fold_in(_rk, 1), 123), (1024,), 23, 99898, jnp.int32), jax.random.randint(jax.random.fold_in(jax.random.fold_in(_rk, 1), 124), (1024,), 97, 99947, jnp.int32), jax.random.randint(jax.random.fold_in(jax.random.fold_in(_rk, 1), 125), (1024,), 278, 99926, jnp.int32), jax.random.randint(jax.random.fold_in(jax.random.fold_in(_rk, 1), 126), (1024,), 64, 12475, jnp.int32), jax.random.randint(jax.random.fold_in(jax.random.fold_in(_rk, 1), 127), (1024,), 51, 99692, jnp.int32), jax.random.randint(jax.random.fold_in(jax.random.fold_in(_rk, 1), 128), (1024,), 89, 99898, jnp.int32), jax.random.randint(jax.random.fold_in(jax.random.fold_in(_rk, 1), 129), (1024,), 91, 99924, jnp.int32), jax.random.randint(jax.random.fold_in(jax.random.fold_in(_rk, 1), 130), (1024,), 140, 99787, jnp.int32), jax.random.randint(jax.random.fold_in(jax.random.fold_in(_rk, 1), 131), (1024,), 243, 99902, jnp.int32), jax.random.randint(jax.random.fold_in(jax.random.fold_in(_rk, 1), 132), (1024,), 15, 99925, jnp.int32), jax.random.randint(jax.random.fold_in(jax.random.fold_in(_rk, 1), 133), (1024,), 64, 12479, jnp.int32), jax.random.randint(jax.random.fold_in(jax.random.fold_in(_rk, 1), 134), (1024,), 68, 99897, jnp.int32), jax.random.randint(jax.random.fold_in(jax.random.fold_in(_rk, 1), 135), (1024,), 48, 99724, jnp.int32), jax.random.randint(jax.random.fold_in(jax.random.fold_in(_rk, 1), 136), (1024,), 69, 99654, jnp.int32), jax.random.randint(jax.random.fold_in(jax.random.fold_in(_rk, 1), 137), (1024,), 13, 99799, jnp.int32), jax.random.randint(jax.random.fold_in(jax.random.fold_in(_rk, 1), 138), (1024,), 37, 12499, jnp.int32), jax.random.randint(jax.random.fold_in(jax.random.fold_in(_rk, 1), 139), (1024,), 77, 99868, jnp.int32), jax.random.randint(jax.random.fold_in(jax.random.fold_in(_rk, 1), 140), (1024,), 16, 12496, jnp.int32), jax.random.randint(jax.random.fold_in(jax.random.fold_in(_rk, 1), 141), (1024,), 433, 99942, jnp.int32), jax.random.randint(jax.random.fold_in(jax.random.fold_in(_rk, 1), 142), (1024,), 37, 99875, jnp.int32), jax.random.randint(jax.random.fold_in(jax.random.fold_in(_rk, 1), 143), (1024,), 18, 99975, jnp.int32), jax.random.randint(jax.random.fold_in(jax.random.fold_in(_rk, 1), 144), (1024,), 54, 99906, jnp.int32), jax.random.randint(jax.random.fold_in(jax.random.fold_in(_rk, 1), 145), (1024,), 19, 99981, jnp.int32), jax.random.randint(jax.random.fold_in(jax.random.fold_in(_rk, 1), 146), (1024,), 67, 99994, jnp.int32), jax.random.randint(jax.random.fold_in(jax.random.fold_in(_rk, 1), 147), (1024,), 88, 99953, jnp.int32), jax.random.randint(jax.random.fold_in(jax.random.fold_in(_rk, 1), 148), (1024,), 14, 99946, jnp.int32), jax.random.randint(jax.random.fold_in(jax.random.fold_in(_rk, 1), 149), (1024,), 161, 99876, jnp.int32), jax.random.randint(jax.random.fold_in(jax.random.fold_in(_rk, 1), 150), (1024,), 106, 99987, jnp.int32), jax.random.randint(jax.random.fold_in(jax.random.fold_in(_rk, 1), 151), (1024,), 57, 12486, jnp.int32), jax.random.randint(jax.random.fold_in(jax.random.fold_in(_rk, 1), 152), (1024,), 2, 12496, jnp.int32), jax.random.randint(jax.random.fold_in(jax.random.fold_in(_rk, 1), 153), (1024,), 77, 12477, jnp.int32), jax.random.randint(jax.random.fold_in(jax.random.fold_in(_rk, 1), 154), (1024,), 2, 99578, jnp.int32), jax.random.randint(jax.random.fold_in(jax.random.fold_in(_rk, 1), 155), (1024,), 96, 99969, jnp.int32), jax.random.randint(jax.random.fold_in(jax.random.fold_in(_rk, 1), 156), (1024,), 114, 99932, jnp.int32), jax.random.randint(jax.random.fold_in(jax.random.fold_in(_rk, 1), 157), (1024,), 9, 99751, jnp.int32), jax.random.randint(jax.random.fold_in(jax.random.fold_in(_rk, 1), 158), (1024,), 92, 99909, jnp.int32), jax.random.randint(jax.random.fold_in(jax.random.fold_in(_rk, 1), 159), (1024,), 10, 12475, jnp.int32), jax.random.randint(jax.random.fold_in(jax.random.fold_in(_rk, 1), 160), (1024,), 48, 99893, jnp.int32), jax.random.randint(jax.random.fold_in(jax.random.fold_in(_rk, 1), 161), (1024,), 57, 99937, jnp.int32), jax.random.randint(jax.random.fold_in(jax.random.fold_in(_rk, 1), 162), (1024,), 15, 99971, jnp.int32), jax.random.randint(jax.random.fold_in(jax.random.fold_in(_rk, 1), 163), (1024,), 27, 12497, jnp.int32), jax.random.randint(jax.random.fold_in(jax.random.fold_in(_rk, 1), 164), (1024,), 226, 99679, jnp.int32), jax.random.randint(jax.random.fold_in(jax.random.fold_in(_rk, 1), 165), (1024,), 249, 99902, jnp.int32), jax.random.randint(jax.random.fold_in(jax.random.fold_in(_rk, 1), 166), (1024,), 122, 99587, jnp.int32), jax.random.randint(jax.random.fold_in(jax.random.fold_in(_rk, 1), 167), (1024,), 511, 99853, jnp.int32), jax.random.randint(jax.random.fold_in(jax.random.fold_in(_rk, 1), 168), (1024,), 207, 99990, jnp.int32), jax.random.randint(jax.random.fold_in(jax.random.fold_in(_rk, 1), 169), (1024,), 65, 99893, jnp.int32), jax.random.randint(jax.random.fold_in(jax.random.fold_in(_rk, 1), 170), (1024,), 127, 99983, jnp.int32), jax.random.randint(jax.random.fold_in(jax.random.fold_in(_rk, 1), 171), (1024,), 10, 99942, jnp.int32), jax.random.randint(jax.random.fold_in(jax.random.fold_in(_rk, 1), 172), (1024,), 14, 99970, jnp.int32), jax.random.randint(jax.random.fold_in(jax.random.fold_in(_rk, 1), 173), (1024,), 97, 99844, jnp.int32), jax.random.randint(jax.random.fold_in(jax.random.fold_in(_rk, 1), 174), (1024,), 211, 99849, jnp.int32), jax.random.randint(jax.random.fold_in(jax.random.fold_in(_rk, 1), 175), (1024,), 111, 12498, jnp.int32), jax.random.randint(jax.random.fold_in(jax.random.fold_in(_rk, 1), 176), (1024,), 141, 99770, jnp.int32), jax.random.randint(jax.random.fold_in(jax.random.fold_in(_rk, 1), 177), (1024,), 32, 99996, jnp.int32), jax.random.randint(jax.random.fold_in(jax.random.fold_in(_rk, 1), 178), (1024,), 74, 99854, jnp.int32), jax.random.randint(jax.random.fold_in(jax.random.fold_in(_rk, 1), 179), (1024,), 27, 12498, jnp.int32), jax.random.randint(jax.random.fold_in(jax.random.fold_in(_rk, 1), 180), (1024,), 91, 99981, jnp.int32), jax.random.randint(jax.random.fold_in(jax.random.fold_in(_rk, 1), 181), (1024,), 141, 99917, jnp.int32), jax.random.randint(jax.random.fold_in(jax.random.fold_in(_rk, 1), 182), (1024,), 40, 12493, jnp.int32), jax.random.randint(jax.random.fold_in(jax.random.fold_in(_rk, 1), 183), (1024,), 31, 99867, jnp.int32), jax.random.randint(jax.random.fold_in(jax.random.fold_in(_rk, 1), 184), (1024,), 122, 99973, jnp.int32), jax.random.randint(jax.random.fold_in(jax.random.fold_in(_rk, 1), 185), (1024,), 149, 99734, jnp.int32), jax.random.randint(jax.random.fold_in(jax.random.fold_in(_rk, 1), 186), (1024,), 222, 99979, jnp.int32), jax.random.randint(jax.random.fold_in(jax.random.fold_in(_rk, 1), 187), (1024,), 69, 99964, jnp.int32), jax.random.randint(jax.random.fold_in(jax.random.fold_in(_rk, 1), 188), (1024,), 72, 99999, jnp.int32), jax.random.randint(jax.random.fold_in(jax.random.fold_in(_rk, 1), 189), (1024,), 237, 99955, jnp.int32), jax.random.randint(jax.random.fold_in(jax.random.fold_in(_rk, 1), 190), (1024,), 1, 12492, jnp.int32), jax.random.randint(jax.random.fold_in(jax.random.fold_in(_rk, 1), 191), (1024,), 42, 12472, jnp.int32), jax.random.randint(jax.random.fold_in(jax.random.fold_in(_rk, 1), 192), (1024,), 64, 99997, jnp.int32), jax.random.randint(jax.random.fold_in(jax.random.fold_in(_rk, 1), 193), (1024,), 36, 12483, jnp.int32), jax.random.randint(jax.random.fold_in(jax.random.fold_in(_rk, 1), 194), (1024,), 55, 99933, jnp.int32), jax.random.randint(jax.random.fold_in(jax.random.fold_in(_rk, 1), 195), (1024,), 122, 99868, jnp.int32), jax.random.randint(jax.random.fold_in(jax.random.fold_in(_rk, 1), 196), (1024,), 119, 99961, jnp.int32), jax.random.randint(jax.random.fold_in(jax.random.fold_in(_rk, 1), 197), (1024,), 152, 99937, jnp.int32), jax.random.randint(jax.random.fold_in(jax.random.fold_in(_rk, 1), 198), (1024,), 20, 99759, jnp.int32), jax.random.randint(jax.random.fold_in(jax.random.fold_in(_rk, 1), 199), (1024,), 27, 99851, jnp.int32)], axis=1)
        r_retrieved_indices = jnp.stack([jax.random.randint(jax.random.fold_in(jax.random.fold_in(_rk, 2), 0), (1024,), 55, 99965, jnp.int32), jax.random.randint(jax.random.fold_in(jax.random.fold_in(_rk, 2), 1), (1024,), 48, 12493, jnp.int32), jax.random.randint(jax.random.fold_in(jax.random.fold_in(_rk, 2), 2), (1024,), 149, 99818, jnp.int32), jax.random.randint(jax.random.fold_in(jax.random.fold_in(_rk, 2), 3), (1024,), 64, 99943, jnp.int32), jax.random.randint(jax.random.fold_in(jax.random.fold_in(_rk, 2), 4), (1024,), 83, 99948, jnp.int32), jax.random.randint(jax.random.fold_in(jax.random.fold_in(_rk, 2), 5), (1024,), 54, 99999, jnp.int32), jax.random.randint(jax.random.fold_in(jax.random.fold_in(_rk, 2), 6), (1024,), 215, 99939, jnp.int32), jax.random.randint(jax.random.fold_in(jax.random.fold_in(_rk, 2), 7), (1024,), 95, 99911, jnp.int32), jax.random.randint(jax.random.fold_in(jax.random.fold_in(_rk, 2), 8), (1024,), 33, 99809, jnp.int32), jax.random.randint(jax.random.fold_in(jax.random.fold_in(_rk, 2), 9), (1024,), 67, 99845, jnp.int32), jax.random.randint(jax.random.fold_in(jax.random.fold_in(_rk, 2), 10), (1024,), 35, 99948, jnp.int32), jax.random.randint(jax.random.fold_in(jax.random.fold_in(_rk, 2), 11), (1024,), 56, 99973, jnp.int32), jax.random.randint(jax.random.fold_in(jax.random.fold_in(_rk, 2), 12), (1024,), 30, 99941, jnp.int32), jax.random.randint(jax.random.fold_in(jax.random.fold_in(_rk, 2), 13), (1024,), 97, 99859, jnp.int32), jax.random.randint(jax.random.fold_in(jax.random.fold_in(_rk, 2), 14), (1024,), 23, 99998, jnp.int32), jax.random.randint(jax.random.fold_in(jax.random.fold_in(_rk, 2), 15), (1024,), 116, 99994, jnp.int32), jax.random.randint(jax.random.fold_in(jax.random.fold_in(_rk, 2), 16), (1024,), 148, 12495, jnp.int32), jax.random.randint(jax.random.fold_in(jax.random.fold_in(_rk, 2), 17), (1024,), 206, 99747, jnp.int32), jax.random.randint(jax.random.fold_in(jax.random.fold_in(_rk, 2), 18), (1024,), 37, 99628, jnp.int32), jax.random.randint(jax.random.fold_in(jax.random.fold_in(_rk, 2), 19), (1024,), 324, 12483, jnp.int32), jax.random.randint(jax.random.fold_in(jax.random.fold_in(_rk, 2), 20), (1024,), 89, 12495, jnp.int32), jax.random.randint(jax.random.fold_in(jax.random.fold_in(_rk, 2), 21), (1024,), 68, 99881, jnp.int32), jax.random.randint(jax.random.fold_in(jax.random.fold_in(_rk, 2), 22), (1024,), 2, 99711, jnp.int32), jax.random.randint(jax.random.fold_in(jax.random.fold_in(_rk, 2), 23), (1024,), 311, 99742, jnp.int32), jax.random.randint(jax.random.fold_in(jax.random.fold_in(_rk, 2), 24), (1024,), 53, 99950, jnp.int32), jax.random.randint(jax.random.fold_in(jax.random.fold_in(_rk, 2), 25), (1024,), 190, 99982, jnp.int32), jax.random.randint(jax.random.fold_in(jax.random.fold_in(_rk, 2), 26), (1024,), 216, 99910, jnp.int32), jax.random.randint(jax.random.fold_in(jax.random.fold_in(_rk, 2), 27), (1024,), 148, 99953, jnp.int32), jax.random.randint(jax.random.fold_in(jax.random.fold_in(_rk, 2), 28), (1024,), 137, 99935, jnp.int32), jax.random.randint(jax.random.fold_in(jax.random.fold_in(_rk, 2), 29), (1024,), 122, 12485, jnp.int32), jax.random.randint(jax.random.fold_in(jax.random.fold_in(_rk, 2), 30), (1024,), 8, 99927, jnp.int32), jax.random.randint(jax.random.fold_in(jax.random.fold_in(_rk, 2), 31), (1024,), 13, 99979, jnp.int32), jax.random.randint(jax.random.fold_in(jax.random.fold_in(_rk, 2), 32), (1024,), 120, 99930, jnp.int32), jax.random.randint(jax.random.fold_in(jax.random.fold_in(_rk, 2), 33), (1024,), 49, 99972, jnp.int32), jax.random.randint(jax.random.fold_in(jax.random.fold_in(_rk, 2), 34), (1024,), 134, 99879, jnp.int32), jax.random.randint(jax.random.fold_in(jax.random.fold_in(_rk, 2), 35), (1024,), 12, 99958, jnp.int32), jax.random.randint(jax.random.fold_in(jax.random.fold_in(_rk, 2), 36), (1024,), 168, 12497, jnp.int32), jax.random.randint(jax.random.fold_in(jax.random.fold_in(_rk, 2), 37), (1024,), 57, 99894, jnp.int32), jax.random.randint(jax.random.fold_in(jax.random.fold_in(_rk, 2), 38), (1024,), 231, 99987, jnp.int32), jax.random.randint(jax.random.fold_in(jax.random.fold_in(_rk, 2), 39), (1024,), 35, 99956, jnp.int32), jax.random.randint(jax.random.fold_in(jax.random.fold_in(_rk, 2), 40), (1024,), 23, 12490, jnp.int32), jax.random.randint(jax.random.fold_in(jax.random.fold_in(_rk, 2), 41), (1024,), 114, 99951, jnp.int32), jax.random.randint(jax.random.fold_in(jax.random.fold_in(_rk, 2), 42), (1024,), 0, 99894, jnp.int32), jax.random.randint(jax.random.fold_in(jax.random.fold_in(_rk, 2), 43), (1024,), 158, 99699, jnp.int32), jax.random.randint(jax.random.fold_in(jax.random.fold_in(_rk, 2), 44), (1024,), 28, 99839, jnp.int32), jax.random.randint(jax.random.fold_in(jax.random.fold_in(_rk, 2), 45), (1024,), 5, 99956, jnp.int32), jax.random.randint(jax.random.fold_in(jax.random.fold_in(_rk, 2), 46), (1024,), 69, 99986, jnp.int32), jax.random.randint(jax.random.fold_in(jax.random.fold_in(_rk, 2), 47), (1024,), 4, 99981, jnp.int32), jax.random.randint(jax.random.fold_in(jax.random.fold_in(_rk, 2), 48), (1024,), 55, 99931, jnp.int32), jax.random.randint(jax.random.fold_in(jax.random.fold_in(_rk, 2), 49), (1024,), 82, 99978, jnp.int32)], axis=1)
        return (r_sequence_ids, r_retrieved_indices)
    r_sequence_ids, r_retrieved_indices = _rec_inputs()

    def _L0_rec_setup():
        import jax, jax.numpy as jnp
        import numpy as np
        N_ITEMS = 12500
        HIDDEN = 512
        BATCH = 1024
        SEQ_LEN = 200
        TOP_K = 50
        key = jax.random.key(seed)
        ks = jax.random.split(key, 9)
        s = 1.0 / np.sqrt(HIDDEN)
        return {'sequence_ids': jax.random.randint(ks[0], (BATCH, SEQ_LEN), 0, N_ITEMS + 1, dtype=jnp.int64 if jax.config.jax_enable_x64 else jnp.int32), 'retrieved_indices': jax.random.randint(ks[1], (BATCH, TOP_K), 0, N_ITEMS, dtype=jnp.int64 if jax.config.jax_enable_x64 else jnp.int32), 'item_embeddings': jax.random.normal(ks[2], (N_ITEMS, HIDDEN), jnp.float32) * 0.02, 'W_rec': jax.random.normal(ks[3], (HIDDEN, HIDDEN), jnp.float32) * s, 'b_rec': jnp.zeros((HIDDEN,), jnp.float32), 'gate_W': jax.random.normal(ks[4], (HIDDEN, 2 * HIDDEN), jnp.float32) * s, 'gate_b': jnp.zeros((HIDDEN,), jnp.float32), 'proj_W': jax.random.normal(ks[5], (N_ITEMS, HIDDEN), jnp.float32) * s, 'proj_b': jnp.zeros((N_ITEMS,), jnp.float32)}
    _L0_rec_all = _L0_rec_setup()
    _L0_rec_in = {k: v for k, v in _L0_rec_all.items() if k in ('item_embeddings', 'W_rec', 'b_rec', 'gate_W', 'gate_b', 'proj_W', 'proj_b')}
    del _L0_rec_all
    return {'r_sequence_ids': r_sequence_ids, 'r_retrieved_indices': r_retrieved_indices, 'L0_rec_item_embeddings': _L0_rec_in['item_embeddings'], 'L0_rec_W_rec': _L0_rec_in['W_rec'], 'L0_rec_b_rec': _L0_rec_in['b_rec'], 'L0_rec_gate_W': _L0_rec_in['gate_W'], 'L0_rec_gate_b': _L0_rec_in['gate_b'], 'L0_rec_proj_W': _L0_rec_in['proj_W'], 'L0_rec_proj_b': _L0_rec_in['proj_b']}

def reference(r_sequence_ids, r_retrieved_indices, L0_rec_item_embeddings, L0_rec_W_rec, L0_rec_b_rec, L0_rec_gate_W, L0_rec_gate_b, L0_rec_proj_W, L0_rec_proj_b):
    import jax
    import jax.numpy as jnp

    def _L0_rec_ref(sequence_ids, retrieved_indices, item_embeddings, W_rec, b_rec, gate_W, gate_b, proj_W, proj_b):
        import jax, jax.numpy as jnp
        import numpy as np
        N_ITEMS = 12500
        HIDDEN = 512
        BATCH = 1024
        SEQ_LEN = 200
        TOP_K = 50
        mask = (sequence_ids != 0)[..., None]
        gathered = item_embeddings[jnp.clip(sequence_ids - 1, 0)]
        seq_emb = jnp.where(mask, gathered, 0.0)
        denom = jnp.maximum(mask.sum(axis=1), 1).astype(seq_emb.dtype)
        pooled = seq_emb.sum(axis=1) / denom
        user_rep = pooled @ W_rec.T + b_rec
        retrieved = item_embeddings[retrieved_indices].mean(axis=1)
        concat = jnp.concatenate([user_rep, retrieved], axis=1)
        gate = jax.nn.sigmoid(concat @ gate_W.T + gate_b)
        fused = gate * user_rep + (1.0 - gate) * retrieved
        logits = fused @ proj_W.T + proj_b
        return logits
    y = _L0_rec_ref(r_sequence_ids, r_retrieved_indices, L0_rec_item_embeddings, L0_rec_W_rec, L0_rec_b_rec, L0_rec_gate_W, L0_rec_gate_b, L0_rec_proj_W, L0_rec_proj_b)
    return y

_drawn_inputs = setup_inputs


def setup_inputs(seed=0):
    import zlib

    import numpy as np

    out = dict(_drawn_inputs(seed))
    spreads = {'L0_rec_b_rec': (0.0, 0.1), 'L0_rec_gate_b': (0.0, 0.344), 'L0_rec_proj_b': (0.0, 0.1)}
    factors = {}
    for name, (base, spread) in spreads.items():
        noise = np.random.default_rng([zlib.crc32(name.encode()), seed]).standard_normal(out[name].shape)
        drawn = base * np.exp(spread * noise) if base else spread * noise
        out[name] = jnp.asarray(drawn.astype(out[name].dtype))
    for name, factor in factors.items():
        out[name] = (out[name] * factor).astype(out[name].dtype)
    return out
```

```python
from contextlib import ExitStack

import concourse.bass as bass
from concourse import mybir

ACT = mybir.ActivationFunctionType
ALU = mybir.AluOpType
AX = mybir.AxisListType
F32 = mybir.dt.float32
F32R = mybir.dt.float32r
F16 = mybir.dt.float16
BF16 = mybir.dt.bfloat16
I32 = mybir.dt.int32

P = 128
BATCH, SEQ, TOPK, ITEMS, HID = 1024, 200, 50, 12500, 512
KT = HID // P
HI = -(-ITEMS // P)
SEQ_B = SEQ - P
ROWS_B = SEQ_B + TOPK
COLS_B = 2 * HI
CHUNK = 256
CHUNKS = BATCH // CHUNK
BT = CHUNK // P
G = 8
GROUPS = CHUNK // G
QUAD = G // 2
E_UNITS = HI // 2
E_LOOPS, E_REST = divmod(E_UNITS, 4)
NCOL = 500
NBLK = ITEMS // NCOL
W_UNITS = 2 * NBLK
PAIRS = NBLK // 2
EARLY = GROUPS - 2 * PAIRS
assert E_REST == 1 and NBLK == 2 * PAIRS + 1 and HI % 2 == 0 and ROWS_B <= P

RAW = 4
E_PER = [sum((u + 2) % RAW == s for u in range(E_UNITS)) for s in range(RAW)]
W_PER = [sum(w % RAW == s for w in range(W_UNITS)) for s in range(RAW)]
EVEN, ODD = PAIRS + 1, PAIRS


def e_loads(c, slot, i):
    return (E_PER[slot] + W_PER[slot]) * c + E_PER[slot] + i + 1


def w_loads(c, slot, i):
    return (E_PER[slot] + W_PER[slot]) * c + 2 * E_PER[slot] + i + 1


def build(nc, ids_a, ids_b, emb, w_rec, b_rec, w_gate, b_gate, w_proj, b_proj, out):
    out_v = out.rearrange("(c b p) n -> c p b n", b=BT, p=P)
    with ExitStack() as ctx:
        def sb(name, shape, dt):
            return ctx.enter_context(nc.sbuf_tensor(name, shape, dt))

        def sem(name):
            return ctx.enter_context(nc.semaphore(name))

        counts = sb("counts", [P, HI, 2 * CHUNK], BF16)
        raw = sb("raw", [P, RAW, 2 * HID], F32)
        e_high = sb("e_high", [P, 4, HID], F16)
        e_low = sb("e_low", [P, 4, HID], F16)
        w_high = sb("w_high", [P, 4, NCOL], F32R)
        w_low = sb("w_low", [P, 4, NCOL], F32R)
        onehot = sb("onehot", [P, 2, (2 * P + HI + COLS_B) * G], BF16)
        ramp = sb("ramp", [P, COLS_B, G], BF16)
        stage = sb("stage", [P, 2, BT, NCOL], F32)
        bias = sb("bias", [P, 2, NCOL], F32)
        wrec_sb = sb("wrec_sb", [P, KT, HID], F32)
        retrieved = sb("retrieved", [P, KT, CHUNK], F32)
        user = sb("user", [P, KT, CHUNK], F32)
        mix_high = sb("mix_high", [P, KT, CHUNK], F32R)
        mix_low = sb("mix_low", [P, KT, CHUNK], F32R)
        ids = sb("ids", [P, 4, BATCH], BF16)
        recip = sb("recip", [P, BATCH], F32)
        ones = sb("ones", [P, P], BF16)
        brec_sb = sb("brec_sb", [P, KT], F32)
        bgate_sb = sb("bgate_sb", [P, KT], F32)
        row = sb("row", [P, 1], I32)
        is_hist = sb("is_hist", [P, 1], F32)
        is_retr = sb("is_retr", [P, 1], F32)
        wrap = sb("wrap", [P, 1], F32)
        hi_off = sb("hi_off", [P, 1], F32)
        abs_sums = sb("abs_sums", [P, E_UNITS], F32)
        abs_own = sb("abs_own", [P, 1], F32)
        abs_all = sb("abs_all", [P, 1], F32)
        exps = sb("exps", [P, 3], I32)
        scale = sb("scale", [P, 1], I32)
        unscale = sb("unscale", [P, 1], I32)
        retr_scale = sb("retr_scale", [P, 1], F32)
        scale_f, unscale_f = scale[:, :].bitcast(F32), unscale[:, :].bitcast(F32)

        pooled = e_high[:, :, :].rearrange("p a b -> p (a b)").bitcast(F32).rearrange("p (k b) -> p k b", k=KT)
        gate = e_low[:, :, :].rearrange("p a b -> p (a b)").bitcast(F32).rearrange("p (k b) -> p k b", k=KT)
        scan_out = [e_low[:, 2 * h:2 * h + 2, :].rearrange("p a b -> p (a b)").bitcast(BF16) for h in range(2)]
        wgate_sb = onehot[:, :, :].rearrange("p a b -> p (a b)")[:, 0:2 * 2 * KT * HID].bitcast(F32)\
            .rearrange("p (k n) -> p k n", k=2 * KT)
        flat = counts[:, :, :].rearrange("p a b -> p (a b)")

        def scratch(n, dt):
            view = flat[:, 2 * BATCH * n:2 * BATCH * (n + 1)]
            return view.bitcast(dt) if dt != BF16 else view[:, 0:BATCH]

        raw_ids = [scratch(0, I32), scratch(1, I32)]
        tmp_f, tmp_t, idx, part_i = scratch(2, F32), scratch(3, F32), scratch(4, I32), scratch(5, I32)
        mask = [scratch(6, BF16), scratch(7, BF16)]

        acc = ctx.enter_context(nc.psum_tensor("acc", [P, 4, 512], F32))
        table = ctx.enter_context(nc.psum_tensor("table", [P, 2, QUAD, 256], F32))

        def onehots(slot):
            at, views = 0, []
            for n in (P, HI, P, COLS_B):
                views.append(onehot[:, slot, at * G:(at + n) * G].rearrange("p (v g) -> p v g", g=G))
                at += n
            return views

        ids_loaded = sem("ids_loaded")
        small_loaded = sem("small_loaded")
        raw_loaded = [sem(f"raw_loaded{s}") for s in range(RAW)]
        gate_loaded = sem("gate_loaded")
        bias_loaded = [sem(f"bias_loaded{s}") for s in range(2)]
        stored = [sem(f"stored{s}") for s in range(2)]
        ramps_ready = sem("ramps_ready")
        dve_step = sem("dve_step")
        masks_ready = sem("masks_ready")
        lengths_ready = sem("lengths_ready")
        scanned = sem("scanned")
        abs_own_ready = sem("abs_own_ready")
        abs_all_ready = sem("abs_all_ready")
        scale_ready = sem("scale_ready")
        onehot_ready = sem("onehot_ready")
        table_ready = sem("table_ready")
        table_taken = sem("table_taken")
        e_high_ready = sem("e_high_ready")
        e_low_ready = sem("e_low_ready")
        e_used = sem("e_used")
        pooled_ready = sem("pooled_ready")
        retr_ready = sem("retr_ready")
        user_done = sem("user_done")
        user_ready = sem("user_ready")
        gate_done = sem("gate_done")
        gate_ready = sem("gate_ready")
        mix_ready = sem("mix_ready")
        w_high_ready = sem("w_high_ready")
        w_low_ready = sem("w_low_ready")
        w_used = sem("w_used")
        logits_taken = sem("logits_taken")

        block = ctx.enter_context(nc.Block())

        @block.sync
        def _(sp):
            sp.dma_start(raw_ids[0], ids_a).then_inc(ids_loaded, 16)
            sp.dma_start(raw_ids[1], ids_b).then_inc(ids_loaded, 16)

            def load_e(u, slot):
                sp.dma_start(raw[:, slot, :], emb[bass.ds(u, 1)].rearrange("a p n -> p (a n)"))\
                    .then_inc(raw_loaded[slot], 16)

            def load_w(w, slot):
                sp.dma_start(raw[:, slot, 0:2 * NCOL], w_proj[bass.ds(w, 1)].rearrange("a p n -> p (a n)"))\
                    .then_inc(raw_loaded[slot], 16)

            def scan_round(i):
                for j in range(RAW):
                    if not isinstance(i, int) or i > 0:
                        sp.wait_ge(scanned, 4 * i + j - 3)
                    load_e(4 * i + j, (j + 2) % RAW)

            def load_embeddings(c, first_chunk):
                for j in range(RAW):
                    if first_chunk and j == 0:
                        sp.wait_ge(scanned, E_UNITS)
                    elif not first_chunk:
                        sp.wait_ge(w_low_ready, 2 * W_UNITS * (c - 1) + 2 * (W_UNITS - 3 + j))
                    load_e(j, (j + 2) % RAW)
                with sp.Fori(1, E_LOOPS) as i:
                    for j in range(RAW):
                        sp.wait_ge(e_low_ready, HI * c + 2 * (4 * i + j - 3))
                        load_e(4 * i + j, (j + 2) % RAW)
                sp.wait_ge(e_low_ready, HI * c + 2 * (E_UNITS - 4))
                load_e(E_UNITS - 1, (E_UNITS + 1) % RAW)

            def load_gate(c):
                sp.wait_ge(table_ready, 2 * GROUPS * (c + 1))
                sp.dma_start(wgate_sb, w_gate).then_inc(gate_loaded, 16)

            def load_projection(c):
                for j in range(RAW):
                    sp.wait_ge(e_low_ready, HI * c + min(2 * (E_UNITS - 2 + j), HI))
                    load_w(j, j)
                with sp.Fori(1, PAIRS) as i:
                    for j in range(RAW):
                        sp.wait_ge(w_low_ready, 2 * W_UNITS * c + 2 * (4 * i + j - 3))
                        load_w(4 * i + j, j)
                for j in range(2):
                    sp.wait_ge(w_low_ready, 2 * W_UNITS * c + 2 * (4 * PAIRS + j - 3))
                    load_w(4 * PAIRS + j, j)

            scan_round(0)
            sp.dma_start(wrec_sb[:, :, :], w_rec).then_inc(small_loaded, 16)
            sp.dma_start(brec_sb[:, :], b_rec).then_inc(small_loaded, 16)
            sp.dma_start(bgate_sb[:, :], b_gate).then_inc(small_loaded, 16)
            with sp.Fori(1, E_LOOPS) as i:
                scan_round(i)
            sp.wait_ge(scanned, E_UNITS - 4)
            load_e(E_UNITS - 1, (E_UNITS + 1) % RAW)
            load_embeddings(0, True)
            load_gate(0)
            with sp.Fori(1, CHUNKS) as c:
                load_projection(c - 1)
                load_embeddings(c, False)
                load_gate(c)
            load_projection(CHUNKS - 1)

        @block.gpsimd
        def _(pool):
            nc.gpsimd.iota(ramp[:, :, :], pattern=[[1, COLS_B], [0, G]], base=0, channel_multiplier=0,
                           allow_small_or_imprecise_dtypes=True).then_inc(ramps_ready, 1)
            nc.gpsimd.iota(row[:, :], pattern=[[0, 1]], base=0, channel_multiplier=1).then_inc(ramps_ready, 1)
            nc.gpsimd.memset(ones[:, :], 1.0).then_inc(ramps_ready, 1)
            pool.wait_ge(abs_own_ready, 1)
            nc.gpsimd.partition_all_reduce(abs_all[:, :], abs_own[:, :], P, bass.bass_isa.ReduceOp.max)\
                .then_inc(abs_all_ready, 1)

            def load_bias(n, slot):
                pool.dma_start(bias[:, slot, :], b_proj[bass.ds(n, 1), :].broadcast_to([P, NCOL]))\
                    .then_inc(bias_loaded[slot], 16)

            def store(c, n, slot):
                pool.wait_ge(logits_taken, NBLK * c + n + 1)
                pool.dma_start(out_v[c, :, :, bass.ds(n * NCOL, NCOL)], stage[:, slot, :, :])\
                    .then_inc(stored[slot], 16)

            with pool.Fori(0, CHUNKS) as c:
                load_bias(0, 0)
                with pool.Fori(0, PAIRS) as i:
                    for j in range(2):
                        load_bias(2 * i + j + 1, (j + 1) % 2)
                        store(c, 2 * i + j, j)
                store(c, NBLK - 1, 0)
            pool.wait_ge(stored[0], 16 * EVEN * CHUNKS)
            pool.wait_ge(stored[1], 16 * ODD * CHUNKS)

        @block.scalar
        def _(act):
            def scan_unit(i, j):
                slot = (j + 2) % RAW
                act.wait_ge(raw_loaded[slot], 16 * (i + 1))
                if not isinstance(i, int) or 4 * i + j >= 2:
                    act.wait_ge(scanned, 4 * i + j - 1)
                nc.scalar.activation(scan_out[j % 2], raw[:, slot, :], ACT.Abs,
                                     accum_out=abs_sums[:, bass.ds(4 * i + j, 1)]).then_inc(scanned, 1)

            def take_tables(c, g, halves=(0, 1)):
                for q in halves:
                    act.wait_ge(table_ready, 2 * (GROUPS * c + g) + q + 1)
                    to = counts[:, :, :].rearrange("p h (w b) -> p w h b", w=2)
                    nc.scalar.activation(
                        to[:, :, :, bass.ds(g * G + q * QUAD, QUAD)],
                        table[:, q, :, 0:COLS_B].rearrange("p b (w h) -> p w h b", w=2),
                        ACT.Copy).then_inc(table_taken, 1)

            def high_e(c, i, j, wait_used):
                slot = (j + 2) % RAW
                act.wait_ge(raw_loaded[slot], 16 * e_loads(c, slot, i))
                for t in range(2):
                    tile = 8 * i + 2 * j + t
                    if wait_used or j >= 2:
                        act.wait_ge(e_used, HI * c + tile - 3)
                    nc.scalar.activation(e_high[:, (2 * j + t) % 4, :], raw[:, slot, t * HID:(t + 1) * HID],
                                         ACT.Copy, scale=scale_f).then_inc(e_high_ready, 1)

            def embeddings(c):
                for j in range(4):
                    high_e(c, 0, j, False)
                with act.Fori(1, E_LOOPS) as i:
                    for j in range(4):
                        high_e(c, i, j, True)
                high_e(c, E_LOOPS, 0, True)

            def mix(c):
                act.wait_ge(e_used, HI * (c + 1))
                for k in range(KT):
                    act.wait_ge(pooled_ready, KT * c + k + 1)
                    nc.scalar.activation(retrieved[:, k, :], acc[:, k, CHUNK:2 * CHUNK], ACT.Copy,
                                         scale=retr_scale[:, :]).then_inc(retr_ready, 1)
                act.wait_ge(small_loaded, 48)
                for o in range(KT):
                    act.wait_ge(user_done, KT * c + o + 1)
                    nc.scalar.activation(user[:, o, :], acc[:, o, 0:CHUNK],
                                         ACT.Identity, bias=brec_sb[:, o:o + 1]).then_inc(user_ready, 1)
                for o in range(KT):
                    act.wait_ge(gate_done, KT * c + o + 1)
                    nc.scalar.activation(gate[:, o, :], acc[:, o, 0:CHUNK],
                                         ACT.Sigmoid, bias=bgate_sb[:, o:o + 1]).then_inc(gate_ready, 1)

            def high_w(c, i, b, wait_used):
                for k in range(KT):
                    slot = 2 * b + k // 2
                    if k % 2 == 0:
                        act.wait_ge(raw_loaded[slot], 16 * w_loads(c, slot, i))
                    if wait_used or b:
                        act.wait_ge(w_used, 2 * W_UNITS * c + 8 * i + 4 * b + k - 3)
                    nc.scalar.activation(w_high[:, k, :], raw[:, slot, k % 2 * NCOL:(k % 2 + 1) * NCOL],
                                         ACT.Copy).then_inc(w_high_ready, 1)

            def logits(c, tables):
                def pair(i, first):
                    for b in range(2):
                        high_w(c, i, b, not first)
                        if tables:
                            take_tables(c + 1, 2 * i + b + EARLY - 1)
                pair(0, True)
                with act.Fori(1, PAIRS) as i:
                    pair(i, False)
                high_w(c, PAIRS, 0, True)
                if tables:
                    take_tables(c + 1, GROUPS - 1)

            act.wait_ge(masks_ready, 1)

            def scan_and_tables(i):
                for g in range(GROUPS // 4):
                    for u in range(g * 12 // 8, (g + 1) * 12 // 8):
                        scan_unit(3 * i + u // 4, u % 4)
                    take_tables(0, 8 * i + g)

            act.wait_ge(lengths_ready, 2)
            scan_and_tables(0)
            with act.Fori(1, 4) as i:
                scan_and_tables(i)
            scan_unit(E_LOOPS, 0)
            act.wait_ge(scale_ready, 1)
            embeddings(0)
            mix(0)
            with act.Fori(1, CHUNKS) as c:
                act.wait_ge(e_used, HI * c)
                with act.Fori(0, EARLY - 1) as g:
                    take_tables(c, g)
                logits(c - 1, True)
                act.wait_ge(mix_ready, c)
                embeddings(c)
                mix(c)
            logits(CHUNKS - 1, False)

        @block.vector
        def _(dve):
            steps = [0]

            def then(ins):
                steps[0] += 1
                ins.then_inc(dve_step, 1)
                dve.wait_ge(dve_step, steps[0])

            def split_ids(n, hist, retr, wrap_by, off):
                x = raw_ids[n]
                then(nc.vector.tensor_scalar(tmp_f, x, 0.0, wrap_by, ALU.is_lt, ALU.mult))
                if n == 0:
                    then(nc.vector.tensor_scalar(tmp_t, x, -1.0, None, ALU.add))
                else:
                    then(nc.vector.scalar_tensor_tensor(tmp_t, x, hist, tmp_f, ALU.subtract, ALU.add))
                then(nc.vector.tensor_scalar(idx, tmp_t, 0.0, float(ITEMS - 1), ALU.max, ALU.min))
                then(nc.vector.tensor_scalar(mask[n], x, 0.0, hist, ALU.not_equal, ALU.mult))
                then(nc.vector.tensor_scalar(part_i, idx, 7, None, ALU.logical_shift_right))
                then(nc.vector.tensor_scalar(ids[:, 2 * n + 1, :], part_i, off, None, ALU.add))
                then(nc.vector.tensor_scalar(part_i, idx, P - 1, None, ALU.bitwise_and))
                then(nc.vector.tensor_scalar(tmp_f, x, 0.0, retr, ALU.not_equal, ALU.max))
                then(nc.vector.scalar_tensor_tensor(tmp_t, part_i, 1.0, tmp_f, ALU.add, ALU.mult))
                then(nc.vector.tensor_scalar(ids[:, 2 * n, :], tmp_t, -1.0, None, ALU.add))

            def make_onehots(c, g, slot, parts=range(4)):
                for n in parts:
                    view = onehots(slot)[n]
                    at = ids[:, n, bass.ds((c * GROUPS + g) * G, G)]
                    ins = nc.vector.tensor_tensor(view, ramp[:, 0:view.shape[1], :],
                                                  at.unsqueeze(1).broadcast_to(list(view.shape)), ALU.is_equal)
                    if n == 3:
                        ins.then_inc(onehot_ready, 1)

            def onehots_free(c, g):
                dve.wait_ge(table_ready, 2 * (GROUPS * c + g) - 2)

            def low_e(c, i, j):
                slot = (j + 2) % RAW
                for t in range(2):
                    s = (2 * j + t) % 4
                    dve.wait_ge(e_high_ready, HI * c + 8 * i + 2 * j + t + 1)
                    nc.vector.scalar_tensor_tensor(e_low[:, s, :], raw[:, slot, t * HID:(t + 1) * HID], scale_f,
                                                   e_high[:, s, :], ALU.mult, ALU.subtract)\
                        .then_inc(e_low_ready, 1)

            def embeddings(c):
                with dve.Fori(0, E_LOOPS) as i:
                    for j in range(4):
                        low_e(c, i, j)
                low_e(c, E_LOOPS, 0)

            def mix(c, chain):
                dve.wait_ge(e_used, HI * (c + 1))
                for k in range(KT):
                    nc.vector.scalar_tensor_tensor(pooled[:, k, :], acc[:, k, 0:CHUNK], unscale_f,
                                                   recip[:, bass.ds(c * CHUNK, CHUNK)], ALU.mult, ALU.mult)\
                        .then_inc(pooled_ready, 1)
                dve.wait_ge(gate_ready, KT * (c + 1))
                chain(nc.vector.tensor_tensor(user[:, :, :], user[:, :, :], retrieved[:, :, :], ALU.subtract), 1)
                chain(nc.vector.tensor_tensor(user[:, :, :], user[:, :, :], gate, ALU.mult), 2)
                chain(nc.vector.tensor_tensor(user[:, :, :], user[:, :, :], retrieved[:, :, :], ALU.add), 3)
                chain(nc.vector.tensor_copy(mix_high[:, :, :], user[:, :, :]), 4)
                nc.vector.tensor_tensor(mix_low[:, :, :], user[:, :, :], mix_high[:, :, :].bitcast(F32),
                                        ALU.subtract).then_inc(mix_ready, 1)

            def low_w(c, i, b, ks):
                for k in ks:
                    dve.wait_ge(w_high_ready, 2 * W_UNITS * c + 8 * i + 4 * b + k + 1)
                    nc.vector.tensor_tensor(w_low[:, k, :], raw[:, 2 * b + k // 2, k % 2 * NCOL:(k % 2 + 1) * NCOL],
                                            w_high[:, k, :].bitcast(F32), ALU.subtract).then_inc(w_low_ready, 1)

            def take_logits(c, i, b, wait_stored):
                dve.wait_ge(w_used, 2 * W_UNITS * c + 4 * (2 * i + b + 1))
                dve.wait_ge(bias_loaded[b], 16 * ((EVEN, ODD)[b] * c + i + 1))
                if wait_stored:
                    dve.wait_ge(stored[b], 16 * ((EVEN, ODD)[b] * c + i))
                nc.vector.tensor_tensor(stage[:, b, :, :], acc[:, 2 * b:2 * b + 2, 0:NCOL],
                                        bias[:, b, :].unsqueeze(1).broadcast_to([P, BT, NCOL]), ALU.add)\
                    .then_inc(logits_taken, 1)

            def logits(c, tables):
                def block_of(i, b, first):
                    g = 2 * i + b + EARLY
                    low_w(c, i, b, (0, 1))
                    if tables:
                        onehots_free(c + 1, g)
                        make_onehots(c + 1, g, b, (0, 1))
                    low_w(c, i, b, (2, 3))
                    if tables:
                        make_onehots(c + 1, g, b, (2, 3))
                    if b:
                        take_logits(c, i, 0, not first)
                    elif not first:
                        take_logits(c, i - 1, 1, True)
                block_of(0, 0, True)
                block_of(0, 1, True)
                low_w(c, 1, 0, (0, 1))
                if tables:
                    onehots_free(c + 1, 2 + EARLY)
                    make_onehots(c + 1, 2 + EARLY, 0, (0, 1))
                low_w(c, 1, 0, (2, 3))
                if tables:
                    make_onehots(c + 1, 2 + EARLY, 0, (2, 3))
                take_logits(c, 0, 1, False)
                block_of(1, 1, False)
                with dve.Fori(2, PAIRS) as i:
                    block_of(i, 0, False)
                    block_of(i, 1, False)
                low_w(c, PAIRS, 0, range(KT))
                take_logits(c, PAIRS - 1, 1, True)
                take_logits(c, PAIRS, 0, True)

            dve.wait_ge(ramps_ready, 3)
            then(nc.vector.tensor_scalar(is_hist[:, :], row[:, :], float(SEQ_B), None, ALU.is_lt))
            then(nc.vector.tensor_scalar(is_retr[:, :], is_hist[:, :], -1.0, 1.0, ALU.mult, ALU.add))
            then(nc.vector.tensor_scalar(wrap[:, :], is_retr[:, :], float(ITEMS), None, ALU.mult))
            then(nc.vector.tensor_scalar(hi_off[:, :], is_retr[:, :], float(HI), None, ALU.mult))
            dve.wait_ge(ids_loaded, 32)
            split_ids(0, 1.0, 0.0, 0.0, 0.0)
            split_ids(1, is_hist[:, :], is_retr[:, :], wrap[:, :], hi_off[:, :])
            nc.vector.tensor_copy(exps[:, 0:1], row[:, :]).then_inc(masks_ready, 1)
            make_onehots(0, 0, 0)
            make_onehots(0, 1, 1)
            for h in range(2):
                cols = recip[:, h * 512:(h + 1) * 512]
                dve.wait_ge(lengths_ready, h + 1)
                then(nc.vector.tensor_scalar(cols, acc[:, h, :], 1.0, None, ALU.max))
                then(nc.vector.reciprocal(cols, cols))
            with dve.Fori(1, GROUPS // 2) as i:
                for j in range(2):
                    onehots_free(0, 2 * i + j)
                    make_onehots(0, 2 * i + j, j)
            dve.wait_ge(scanned, E_UNITS)
            nc.vector.tensor_reduce(abs_own[:, :], abs_sums[:, :], AX.X, ALU.max).then_inc(abs_own_ready, 1)
            dve.wait_ge(abs_all_ready, 1)
            then(nc.vector.tensor_scalar(exps[:, 0:1], abs_all[:, :].bitcast(I32), 23, None,
                                         ALU.logical_shift_right))
            then(nc.vector.tensor_scalar(exps[:, 1:2], exps[:, 0:1], -1.0, 268.0, ALU.mult, ALU.add))
            then(nc.vector.tensor_scalar(exps[:, 0:1], exps[:, 1:2], 1.0, 253.0, ALU.max, ALU.min))
            then(nc.vector.tensor_scalar(exps[:, 2:3], exps[:, 0:1], -1.0, 254.0, ALU.mult, ALU.add))
            then(nc.vector.tensor_scalar(scale[:, :], exps[:, 0:1], 23, None, ALU.logical_shift_left))
            then(nc.vector.tensor_scalar(unscale[:, :], exps[:, 2:3], 23, None, ALU.logical_shift_left))
            nc.vector.tensor_scalar(retr_scale[:, :], unscale_f, 1.0 / TOPK, None, ALU.mult)\
                .then_inc(scale_ready, 1)
            embeddings(0)
            mix(0, lambda ins, n: then(ins))
            base = steps[0]

            with dve.Fori(1, CHUNKS) as c:
                with dve.Fori(0, EARLY // 2) as i:
                    for j in range(2):
                        onehots_free(c, 2 * i + j)
                        make_onehots(c, 2 * i + j, j)
                logits(c - 1, True)
                embeddings(c)

                def chain(ins, n):
                    ins.then_inc(dve_step, 1)
                    dve.wait_ge(dve_step, base + 4 * (c - 1) + n)
                mix(c, chain)
                dve.wait_ge(stored[0], 16 * EVEN * c)
                dve.wait_ge(stored[1], 16 * ODD * c)
            logits(CHUNKS - 1, False)

        @block.tensor
        def _(pe):
            def lengths():
                pe.wait_ge(masks_ready, 1)
                for h in range(2):
                    nc.tensor.matmul(acc[:, h, :], ones[:, :], mask[0][:, h * 512:(h + 1) * 512],
                                     start=True, stop=False)
                    nc.tensor.matmul(acc[:, h, :], ones[:, :], mask[1][:, h * 512:(h + 1) * 512],
                                     start=False, stop=True).then_inc(lengths_ready, 1)

            def tables(c, g, slot, wait_taken=True):
                a_lo, a_hi, b_lo, b_hi = onehots(slot)
                pe.wait_ge(onehot_ready, GROUPS * c + g + 1)
                for q in range(2):
                    if wait_taken:
                        pe.wait_ge(table_taken, 2 * (GROUPS * c + g) + q - 1)
                    for j in range(QUAD):
                        u = q * QUAD + j
                        nc.tensor.matmul(table[:, q, j, 0:COLS_B], b_lo[0:ROWS_B, :, u], b_hi[0:ROWS_B, :, u],
                                         start=True, stop=False)
                        last = nc.tensor.matmul(table[:, q, j, 0:HI], a_lo[:, :, u], a_hi[:, :, u],
                                                start=False, stop=True)
                    last.then_inc(table_ready, 1)

            def sum_tile(c, i, j, first, final):
                tile = 8 * i + j
                pe.wait_ge(e_low_ready, HI * c + tile + 1)
                for k in range(KT):
                    for part in (e_high, e_low):
                        last = nc.tensor.matmul(
                            acc[:, k, :], part[:, j % 4, k * P:(k + 1) * P],
                            counts[:, bass.ds(tile, 1), :].rearrange("p a b -> p (a b)"),
                            start=first and part is e_high, stop=final and part is e_low)
                last.then_inc(e_used, 1)

            def sums(c):
                pe.wait_ge(table_taken, 2 * GROUPS * (c + 1))
                for j in range(8):
                    sum_tile(c, 0, j, j == 0, False)
                with pe.Fori(1, E_LOOPS) as i:
                    for j in range(8):
                        sum_tile(c, i, j, False, False)
                sum_tile(c, E_LOOPS, 0, False, False)
                sum_tile(c, E_LOOPS, 1, False, True)

            def mix(c):
                pe.wait_ge(small_loaded, 48)
                pe.wait_ge(pooled_ready, KT * (c + 1))
                pe.wait_ge(retr_ready, KT * (c + 1))
                for o in range(KT):
                    to = acc[:, o, 0:CHUNK]
                    for k in range(KT):
                        last = nc.tensor.matmul(to, wrec_sb[:, k, o * P:(o + 1) * P], pooled[:, k, :],
                                                start=k == 0, stop=k == KT - 1)
                    last.then_inc(user_done, 1)
                pe.wait_ge(gate_loaded, 16 * (c + 1))
                pe.wait_ge(user_ready, KT * (c + 1))
                for o in range(KT):
                    to = acc[:, o, 0:CHUNK]
                    for k in range(2 * KT):
                        rhs = user[:, k, :] if k < KT else retrieved[:, k - KT, :]
                        last = nc.tensor.matmul(to, wgate_sb[:, k, o * P:(o + 1) * P], rhs,
                                                start=k == 0, stop=k == 2 * KT - 1)
                    last.then_inc(gate_done, 1)

            def logits_block(c, i, b, wait_taken):
                if wait_taken:
                    pe.wait_ge(logits_taken, NBLK * c + 2 * i + b - 1)
                for k in range(KT):
                    pe.wait_ge(w_low_ready, 2 * W_UNITS * c + 8 * i + 4 * b + k + 1)
                    for t in range(BT):
                        to = acc[:, 2 * b + t, 0:NCOL]
                        high, low = (m[:, k, t * P:(t + 1) * P] for m in (mix_high, mix_low))
                        nc.tensor.matmul(to, high, w_high[:, k, :], start=k == 0, stop=False)
                        nc.tensor.matmul(to, high, w_low[:, k, :], start=False, stop=False)
                        last = nc.tensor.matmul(to, low, w_high[:, k, :], start=False, stop=k == KT - 1)
                    last.then_inc(w_used, 1)

            def logits(c, with_tables):
                pe.wait_ge(mix_ready, c + 1)

                def pair(i, first):
                    for b in range(2):
                        logits_block(c, i, b, not first)
                        if with_tables:
                            tables(c + 1, 2 * i + b + EARLY, b)
                pair(0, True)
                with pe.Fori(1, PAIRS) as i:
                    pair(i, False)
                logits_block(c, PAIRS, 0, True)

            lengths()
            tables(0, 0, 0, False)
            tables(0, 1, 1)
            with pe.Fori(1, GROUPS // 2) as i:
                tables(0, 2 * i, 0)
                tables(0, 2 * i + 1, 1)
            sums(0)
            mix(0)
            with pe.Fori(1, CHUNKS) as c:
                with pe.Fori(0, EARLY // 2) as i:
                    tables(c, 2 * i, 0)
                    tables(c, 2 * i + 1, 1)
                logits(c - 1, True)
                pe.wait_ge(logits_taken, NBLK * c)
                sums(c)
                mix(c)
            logits(CHUNKS - 1, False)


def kernel(**inputs):
    import numpy as np
    import concourse.bacc as bacc
    from concourse.bass_utils import run_bass_kernel_spmd

    x = {k: np.asarray(v) for k, v in inputs.items()}
    seq, retr = x["r_sequence_ids"], x["r_retrieved_indices"]
    ids_a = np.ascontiguousarray(seq[:, :P].T)
    ids_b = np.zeros((P, BATCH), seq.dtype)
    ids_b[:SEQ_B] = seq[:, P:].T
    ids_b[SEQ_B:ROWS_B] = retr.T
    emb = x["L0_rec_item_embeddings"]
    emb_p = np.zeros((HI * P, HID), emb.dtype)
    emb_p[:ITEMS] = emb
    emb_p = np.ascontiguousarray(emb_p.reshape(E_UNITS, 2, P, HID).transpose(0, 2, 1, 3)).reshape(E_UNITS, P, 2 * HID)
    w_rec = np.ascontiguousarray(x["L0_rec_W_rec"].T.reshape(KT, P, HID).transpose(1, 0, 2))
    w_gate = np.ascontiguousarray(x["L0_rec_gate_W"].T.reshape(2 * KT, P, HID).transpose(1, 0, 2))
    w_proj = x["L0_rec_proj_W"].T.reshape(2, 2, P, NBLK, NCOL).transpose(3, 0, 2, 1, 4)
    w_proj = np.ascontiguousarray(w_proj).reshape(W_UNITS, P, 2 * NCOL)
    arrays = {
        "ids_a": ids_a, "ids_b": ids_b, "emb": emb_p, "w_rec": w_rec,
        "b_rec": np.ascontiguousarray(x["L0_rec_b_rec"].reshape(KT, P).T), "w_gate": w_gate,
        "b_gate": np.ascontiguousarray(x["L0_rec_gate_b"].reshape(KT, P).T), "w_proj": w_proj,
        "b_proj": np.ascontiguousarray(x["L0_rec_proj_b"].reshape(NBLK, NCOL)),
    }
    nc = bacc.Bacc("TRN2", target_bir_lowering=False, num_devices=1)
    args = [nc.dram_tensor(n, a.shape, mybir.dt.from_np(a.dtype), kind="ExternalInput").ap() for n, a in arrays.items()]
    out = nc.dram_tensor("logits", (BATCH, ITEMS), F32, kind="ExternalOutput").ap()
    build(nc, *args, out)
    r = run_bass_kernel_spmd(nc, [arrays], core_ids=[0])
    return r.results[0]["logits"]
```

```python
from contextlib import ExitStack

import concourse.bass as bass
from concourse import mybir

ACT = mybir.ActivationFunctionType
ALU = mybir.AluOpType
AX = mybir.AxisListType
F32 = mybir.dt.float32
F32R = mybir.dt.float32r
F16 = mybir.dt.float16
BF16 = mybir.dt.bfloat16
I32 = mybir.dt.int32

P = 128
BATCH, SEQ, TOPK, ITEMS, HID = 1024, 200, 50, 12500, 512
KT = HID // P
HI = -(-ITEMS // P)
SEQ_B = SEQ - P
ROWS_B = SEQ_B + TOPK
COLS_B = 2 * HI
CHUNK = 256
CHUNKS = BATCH // CHUNK
BT = CHUNK // P
G = 8
GROUPS = CHUNK // G
QUAD = G // 2
E_UNITS = HI // 2
E_LOOPS, E_REST = divmod(E_UNITS, 4)
NCOL = 500
NBLK = ITEMS // NCOL
W_UNITS = 2 * NBLK
PAIRS = NBLK // 2
EARLY = GROUPS - 2 * PAIRS
assert E_REST == 1 and NBLK == 2 * PAIRS + 1 and HI % 2 == 0 and ROWS_B <= P

RAW = 4
E_PER = [sum((u + 2) % RAW == s for u in range(E_UNITS)) for s in range(RAW)]
W_PER = [sum(w % RAW == s for w in range(W_UNITS)) for s in range(RAW)]
EVEN, ODD = PAIRS + 1, PAIRS


def e_loads(c, slot, i):
    return (E_PER[slot] + W_PER[slot]) * c + E_PER[slot] + i + 1


def w_loads(c, slot, i):
    return (E_PER[slot] + W_PER[slot]) * c + 2 * E_PER[slot] + i + 1


STEPS = 4 * KT + 2 + 8 + 9


def build(nc, ids_a, ids_b, emb, w_rec, b_rec, w_gate, b_gate, w_proj, b_proj, out):
    out_v = out.rearrange("(c b p) n -> c p b n", b=BT, p=P)
    with ExitStack() as ctx:
        def sb(name, shape, dt):
            return ctx.enter_context(nc.sbuf_tensor(name, shape, dt))

        def sem(name):
            return ctx.enter_context(nc.semaphore(name))

        counts = sb("counts", [P, HI, 2 * CHUNK], BF16)
        raw = sb("raw", [P, RAW, 2 * HID], F32)
        e_high = sb("e_high", [P, 4, HID], F16)
        e_low = sb("e_low", [P, 4, HID], F16)
        w_high = sb("w_high", [P, 4, NCOL], F32R)
        w_low = sb("w_low", [P, 4, NCOL], F32R)
        onehot = sb("onehot", [P, 2, (2 * P + HI + COLS_B) * G], BF16)
        ramp = sb("ramp", [P, COLS_B, G], BF16)
        stage_mem = sb("stage_mem", [P, KT * HID], F32)
        bias_mem = sb("bias_mem", [P, KT * CHUNK], F32)
        wrec_sb = sb("wrec_sb", [P, KT, HID], F32)
        wgate_user = sb("wgate_user", [P, KT, HID], F32)
        user = sb("user", [P, KT, CHUNK], F32)
        mix_high = sb("mix_high", [P, KT, CHUNK], F32R)
        mix_low = sb("mix_low", [P, KT, CHUNK], F32R)
        raw_ids = sb("raw_ids", [P, 2, CHUNK], I32)
        ids = sb("ids", [P, 4, CHUNK], BF16)
        mask = sb("mask", [P, 2, CHUNK], BF16)
        recip = sb("recip", [P, CHUNK], F32)
        ones = sb("ones", [P, P], BF16)
        brec_sb = sb("brec_sb", [P, KT], F32)
        bgate_sb = sb("bgate_sb", [P, KT], F32)
        row = sb("row", [P, 1], I32)
        is_hist = sb("is_hist", [P, 1], F32)
        is_retr = sb("is_retr", [P, 1], F32)
        wrap = sb("wrap", [P, 1], F32)
        hi_off = sb("hi_off", [P, 1], F32)
        abs_sums = sb("abs_sums", [P, E_UNITS], F32)
        abs_own = sb("abs_own", [P, 1], F32)
        abs_all = sb("abs_all", [P, 1], F32)
        exps = sb("exps", [P, 3], I32)
        scale = sb("scale", [P, 1], I32)
        unscale = sb("unscale", [P, 1], I32)
        retr_scale = sb("retr_scale", [P, 1], F32)
        scale_f, unscale_f = scale[:, :].bitcast(F32), unscale[:, :].bitcast(F32)

        def flat(t):
            return t[:, :, :].rearrange("p a b -> p (a b)")

        def by_tile(view):
            return view.rearrange("p (k b) -> p k b", k=KT)

        pooled = by_tile(flat(e_high).bitcast(F32))
        gate = by_tile(flat(e_low).bitcast(F32))
        scan_out = [e_low[:, 2 * h:2 * h + 2, :].rearrange("p a b -> p (a b)").bitcast(BF16) for h in range(2)]
        stage = stage_mem[:, 0:2 * BT * NCOL].rearrange("p (s b n) -> p s b n", s=2, b=BT)
        wgate_retr = stage_mem[:, :].rearrange("p (k n) -> p k n", k=KT)
        bias = bias_mem[:, 0:2 * NCOL].rearrange("p (s n) -> p s n", s=2)
        retrieved = by_tile(bias_mem[:, :])
        tmp_f, tmp_t = user[:, 0, :], user[:, 1, :]
        idx, part_i = user[:, 2, :].bitcast(I32), user[:, 3, :].bitcast(I32)

        acc = ctx.enter_context(nc.psum_tensor("acc", [P, 4, 512], F32))
        table = ctx.enter_context(nc.psum_tensor("table", [P, 2, QUAD, 256], F32))
        lengths = table[:, 0, 0, 0:CHUNK]

        def onehots(slot):
            at, views = 0, []
            for n in (P, HI, P, COLS_B):
                views.append(onehot[:, slot, at * G:(at + n) * G].rearrange("p (v g) -> p v g", g=G))
                at += n
            return views

        ids_loaded = sem("ids_loaded")
        small_loaded = sem("small_loaded")
        raw_loaded = [sem(f"raw_loaded{s}") for s in range(RAW)]
        gate_loaded = sem("gate_loaded")
        bias_loaded = [sem(f"bias_loaded{s}") for s in range(2)]
        stored = [sem(f"stored{s}") for s in range(2)]
        ramps_ready = sem("ramps_ready")
        dve_step = sem("dve_step")
        ids_ready = sem("ids_ready")
        lengths_ready = sem("lengths_ready")
        scanned = sem("scanned")
        abs_own_ready = sem("abs_own_ready")
        abs_all_ready = sem("abs_all_ready")
        scale_ready = sem("scale_ready")
        onehot_ready = sem("onehot_ready")
        table_ready = sem("table_ready")
        table_taken = sem("table_taken")
        e_high_ready = sem("e_high_ready")
        e_low_ready = sem("e_low_ready")
        e_used = sem("e_used")
        pooled_ready = sem("pooled_ready")
        retr_ready = sem("retr_ready")
        user_done = sem("user_done")
        user_ready = sem("user_ready")
        gate_done = sem("gate_done")
        gate_ready = sem("gate_ready")
        mix_ready = sem("mix_ready")
        w_high_ready = sem("w_high_ready")
        w_low_ready = sem("w_low_ready")
        w_used = sem("w_used")
        logits_taken = sem("logits_taken")

        block = ctx.enter_context(nc.Block())

        @block.sync
        def _(sp):
            def load_ids(c):
                if not isinstance(c, int) or c > 0:
                    sp.wait_ge(ids_ready, c)
                for n, src in enumerate((ids_a, ids_b)):
                    sp.dma_start(raw_ids[:, n, :], src[:, bass.ds(c * CHUNK, CHUNK)]).then_inc(ids_loaded, 16)

            def load_e(u, slot):
                sp.dma_start(raw[:, slot, :], emb[bass.ds(u, 1)].rearrange("a p n -> p (a n)"))\
                    .then_inc(raw_loaded[slot], 16)

            def load_w(w, slot):
                sp.dma_start(raw[:, slot, 0:2 * NCOL], w_proj[bass.ds(w, 1)].rearrange("a p n -> p (a n)"))\
                    .then_inc(raw_loaded[slot], 16)

            def load_bias(n, slot):
                sp.dma_start(bias[:, slot, :], b_proj[bass.ds(n, 1), :].broadcast_to([P, NCOL]))\
                    .then_inc(bias_loaded[slot], 16)

            def store(c, n, slot):
                sp.wait_ge(logits_taken, NBLK * c + n + 1)
                sp.dma_start(out_v[c, :, :, bass.ds(n * NCOL, NCOL)], stage[:, slot, :, :])\
                    .then_inc(stored[slot], 16)

            def scan_round(i):
                for j in range(RAW):
                    if not isinstance(i, int) or i > 0:
                        sp.wait_ge(scanned, 4 * i + j - 3)
                    load_e(4 * i + j, (j + 2) % RAW)

            def first_embeddings(c):
                for j in range(RAW):
                    if not isinstance(c, int) or c > 0:
                        sp.wait_ge(w_low_ready, 2 * W_UNITS * (c - 1) + 2 * (W_UNITS - 3 + j))
                    elif j == 0:
                        sp.wait_ge(scanned, E_UNITS)
                    load_e(j, (j + 2) % RAW)

            def other_embeddings(c):
                with sp.Fori(1, E_LOOPS) as i:
                    for j in range(RAW):
                        sp.wait_ge(e_low_ready, HI * c + 2 * (4 * i + j - 3))
                        load_e(4 * i + j, (j + 2) % RAW)
                sp.wait_ge(e_low_ready, HI * c + 2 * (E_UNITS - 4))
                load_e(E_UNITS - 1, (E_UNITS + 1) % RAW)

            def load_gate(c):
                again = not isinstance(c, int) or c > 0
                if again:
                    sp.wait_ge(gate_done, KT * c)
                sp.dma_start(wgate_user[:, 0:2, :], w_gate[:, 0:2, :]).then_inc(gate_loaded, 16)
                if again:
                    sp.wait_ge(stored[0], 16 * EVEN * c)
                sp.dma_start(wgate_user[:, 2:4, :], w_gate[:, 2:4, :]).then_inc(gate_loaded, 16)
                if again:
                    sp.wait_ge(stored[1], 16 * ODD * c)
                sp.dma_start(wgate_retr, w_gate[:, KT:2 * KT, :]).then_inc(gate_loaded, 16)

            def first_projection(c):
                for j in range(RAW):
                    sp.wait_ge(e_low_ready, HI * c + min(2 * (E_UNITS - 2 + j), HI))
                    load_w(j, j)

            def logits(c):
                def load_block(i, b):
                    for h in range(2):
                        sp.wait_ge(w_low_ready, 2 * W_UNITS * c + 2 * (4 * i + 2 * b + h - 3))
                        load_w(4 * i + 2 * b + h, 2 * b + h)

                load_block(1, 0)
                sp.wait_ge(mix_ready, KT * (c + 1))
                load_bias(0, 0)
                load_bias(1, 1)
                with sp.Fori(1, PAIRS) as i:
                    for b in range(2):
                        load_block(i + b, 1 - b)
                        store(c, 2 * i - 2 + b, b)
                        load_bias(2 * i + b, b)
                store(c, NBLK - 3, 0)
                load_bias(NBLK - 1, 0)

            def last_stores(c):
                store(c, NBLK - 2, 1)
                store(c, NBLK - 1, 0)

            def turn(c, more):
                logits(c - 1)
                first_embeddings(c)
                last_stores(c - 1)
                if more:
                    load_ids(c + 1)
                other_embeddings(c)
                load_gate(c)
                first_projection(c)

            load_ids(0)
            scan_round(0)
            sp.dma_start(wrec_sb[:, :, :], w_rec).then_inc(small_loaded, 16)
            sp.dma_start(brec_sb[:, :], b_rec).then_inc(small_loaded, 16)
            sp.dma_start(bgate_sb[:, :], b_gate).then_inc(small_loaded, 16)
            with sp.Fori(1, E_LOOPS) as i:
                scan_round(i)
            sp.wait_ge(scanned, E_UNITS - 4)
            load_e(E_UNITS - 1, (E_UNITS + 1) % RAW)
            first_embeddings(0)
            load_ids(1)
            other_embeddings(0)
            load_gate(0)
            first_projection(0)
            with sp.Fori(1, CHUNKS - 1) as c:
                turn(c, True)
            turn(CHUNKS - 1, False)
            logits(CHUNKS - 1)
            last_stores(CHUNKS - 1)
            sp.wait_ge(stored[0], 16 * EVEN * CHUNKS)
            sp.wait_ge(stored[1], 16 * ODD * CHUNKS)

        @block.gpsimd
        def _(pool):
            nc.gpsimd.iota(row[:, :], pattern=[[0, 1]], base=0, channel_multiplier=1).then_inc(ramps_ready, 1)
            nc.gpsimd.iota(ramp[:, :, :], pattern=[[1, COLS_B], [0, G]], base=0, channel_multiplier=0,
                           allow_small_or_imprecise_dtypes=True).then_inc(ramps_ready, 1)
            nc.gpsimd.memset(ones[:, :], 1.0).then_inc(ramps_ready, 1)
            pool.wait_ge(abs_own_ready, 1)
            nc.gpsimd.partition_all_reduce(abs_all[:, :], abs_own[:, :], P, bass.bass_isa.ReduceOp.max)\
                .then_inc(abs_all_ready, 1)

        @block.scalar
        def _(act):
            def scan_unit(i, j):
                slot = (j + 2) % RAW
                act.wait_ge(raw_loaded[slot], 16 * (i + 1))
                if not isinstance(i, int) or 4 * i + j >= 2:
                    act.wait_ge(scanned, 4 * i + j - 1)
                nc.scalar.activation(scan_out[j % 2], raw[:, slot, :], ACT.Abs,
                                     accum_out=abs_sums[:, bass.ds(4 * i + j, 1)]).then_inc(scanned, 1)

            def take_tables(c, g):
                for q in range(2):
                    act.wait_ge(table_ready, 2 * (GROUPS * c + g) + q + 1)
                    to = counts[:, :, :].rearrange("p h (w b) -> p w h b", w=2)
                    nc.scalar.activation(
                        to[:, :, :, bass.ds(g * G + q * QUAD, QUAD)],
                        table[:, q, :, 0:COLS_B].rearrange("p b (w h) -> p w h b", w=2),
                        ACT.Copy).then_inc(table_taken, 1)

            def high_e(c, i, j, wait_used):
                slot = (j + 2) % RAW
                act.wait_ge(raw_loaded[slot], 16 * e_loads(c, slot, i))
                for t in range(2):
                    tile = 8 * i + 2 * j + t
                    if wait_used or j >= 2:
                        act.wait_ge(e_used, HI * c + tile - 3)
                    nc.scalar.activation(e_high[:, (2 * j + t) % 4, :], raw[:, slot, t * HID:(t + 1) * HID],
                                         ACT.Copy, scale=scale_f).then_inc(e_high_ready, 1)

            def sums(c):
                for j in range(4):
                    high_e(c, 0, j, False)
                with act.Fori(1, E_LOOPS) as i:
                    for j in range(4):
                        high_e(c, i, j, True)
                high_e(c, E_LOOPS, 0, True)

            def high_w(c, i, b, wait_used):
                for k in range(KT):
                    slot = 2 * b + k // 2
                    if k % 2 == 0:
                        act.wait_ge(raw_loaded[slot], 16 * w_loads(c, slot, i))
                    if wait_used:
                        act.wait_ge(w_used, 2 * W_UNITS * c + 8 * i + 4 * b + k - 3)
                    nc.scalar.activation(w_high[:, k, :], raw[:, slot, k % 2 * NCOL:(k % 2 + 1) * NCOL],
                                         ACT.Copy).then_inc(w_high_ready, 1)

            def mix(c, tables):
                act.wait_ge(e_used, HI * (c + 1))
                for k in range(KT):
                    act.wait_ge(pooled_ready, KT * c + k + 1)
                    nc.scalar.activation(retrieved[:, k, :], acc[:, k, CHUNK:2 * CHUNK], ACT.Copy,
                                         scale=retr_scale[:, :]).then_inc(retr_ready, 1)
                if tables:
                    take_tables(c + 1, 0)
                    take_tables(c + 1, 1)
                act.wait_ge(small_loaded, 48)
                for o in range(KT):
                    act.wait_ge(user_done, KT * c + o + 1)
                    nc.scalar.activation(user[:, o, :], acc[:, o, 0:CHUNK], ACT.Identity,
                                         bias=brec_sb[:, o:o + 1]).then_inc(user_ready, 1)
                high_w(c, 0, 0, False)
                for o in range(KT):
                    if tables:
                        take_tables(c + 1, o + 2)
                    act.wait_ge(gate_done, KT * c + o + 1)
                    nc.scalar.activation(gate[:, o, :], acc[:, o, 0:CHUNK], ACT.Sigmoid,
                                         bias=bgate_sb[:, o:o + 1]).then_inc(gate_ready, 1)
                if tables:
                    take_tables(c + 1, 6)

            def logits(c, tables):
                def block_of(i, b, split):
                    if split:
                        high_w(c, i, b, True)
                    if tables:
                        take_tables(c + 1, 2 * i + b + EARLY - 1)
                block_of(0, 0, False)
                block_of(0, 1, True)
                with act.Fori(1, PAIRS) as i:
                    block_of(i, 0, True)
                    block_of(i, 1, True)
                high_w(c, PAIRS, 0, True)
                if tables:
                    take_tables(c + 1, GROUPS - 1)

            def turn(c):
                mix(c - 1, True)
                logits(c - 1, True)
                act.wait_ge(mix_ready, KT * c)
                sums(c)

            def scan_and_tables(i):
                for g in range(GROUPS // 4):
                    for u in range(g * 12 // 8, (g + 1) * 12 // 8):
                        scan_unit(3 * i + u // 4, u % 4)
                    take_tables(0, 8 * i + g)

            scan_and_tables(0)
            with act.Fori(1, 4) as i:
                scan_and_tables(i)
            scan_unit(E_LOOPS, 0)
            act.wait_ge(scale_ready, 1)
            sums(0)
            with act.Fori(1, CHUNKS - 1) as c:
                turn(c)
            turn(CHUNKS - 1)
            mix(CHUNKS - 1, False)
            logits(CHUNKS - 1, False)

        @block.vector
        def _(dve):
            base, taken = [0], [0]

            def then(ins):
                taken[0] += 1
                ins.then_inc(dve_step, 1)
                dve.wait_ge(dve_step, base[0] + taken[0])

            def split_ids(n, hist, retr, wrap_by, off):
                x = raw_ids[:, n, :]
                if n == 0:
                    then(nc.vector.tensor_scalar(tmp_t, x, -1.0, None, ALU.add))
                else:
                    then(nc.vector.tensor_scalar(tmp_f, x, 0.0, wrap_by, ALU.is_lt, ALU.mult))
                    then(nc.vector.scalar_tensor_tensor(tmp_t, x, hist, tmp_f, ALU.subtract, ALU.add))
                then(nc.vector.tensor_scalar(idx, tmp_t, 0.0, float(ITEMS - 1), ALU.max, ALU.min))
                nc.vector.tensor_scalar(mask[:, n, :], x, 0.0, hist, ALU.not_equal, ALU.mult)
                then(nc.vector.tensor_scalar(part_i, idx, 7, None, ALU.logical_shift_right))
                then(nc.vector.tensor_scalar(ids[:, 2 * n + 1, :], part_i, off, None, ALU.add))
                then(nc.vector.tensor_scalar(tmp_f, x, 0.0, retr, ALU.not_equal, ALU.max))
                then(nc.vector.tensor_scalar(part_i, idx, P - 1, None, ALU.bitwise_and))
                then(nc.vector.scalar_tensor_tensor(tmp_t, part_i, 1.0, tmp_f, ALU.add, ALU.mult))
                then(nc.vector.tensor_scalar(ids[:, 2 * n, :], tmp_t, -1.0, None, ALU.add))

            def split_a(c):
                dve.wait_ge(ids_loaded, 32 * (c + 1))
                split_ids(0, 1.0, 0.0, 0.0, 0.0)

            def split_b():
                split_ids(1, is_hist[:, :], is_retr[:, :], wrap[:, :], hi_off[:, :])
                nc.vector.tensor_copy(exps[:, 0:1], row[:, :]).then_inc(ids_ready, 1)

            def make_onehots(c, g, slot, parts=range(4), free=True):
                if free and parts[0] == 0:
                    dve.wait_ge(table_ready, 2 * (GROUPS * c + g) - 2)
                for n in parts:
                    view = onehots(slot)[n]
                    at = ids[:, n, bass.ds(g * G, G)]
                    ins = nc.vector.tensor_tensor(view, ramp[:, 0:view.shape[1], :],
                                                  at.unsqueeze(1).broadcast_to(list(view.shape)), ALU.is_equal)
                    if n == 3:
                        ins.then_inc(onehot_ready, 1)

            def low_e(c, i, j):
                slot = (j + 2) % RAW
                for t in range(2):
                    s = (2 * j + t) % 4
                    dve.wait_ge(e_high_ready, HI * c + 8 * i + 2 * j + t + 1)
                    nc.vector.scalar_tensor_tensor(e_low[:, s, :], raw[:, slot, t * HID:(t + 1) * HID], scale_f,
                                                   e_high[:, s, :], ALU.mult, ALU.subtract)\
                        .then_inc(e_low_ready, 1)

            def sums(c, more, begun):
                def a_round(i):
                    for j in range(4):
                        low_e(c, i, j)

                for j in range(2 if begun else 0, 4):
                    low_e(c, 0, j)
                dve.wait_ge(lengths_ready, c + 1)
                then(nc.vector.tensor_scalar(recip[:, :], lengths, 1.0, None, ALU.max))
                then(nc.vector.reciprocal(recip[:, :], recip[:, :]))
                if more:
                    a_round(1)
                    split_a(c + 1)
                    a_round(2)
                    split_b()
                    a_round(3)
                    make_onehots(c + 1, 0, 0)
                    a_round(4)
                    make_onehots(c + 1, 1, 1)
                with dve.Fori(5 if more else 1, E_LOOPS) as i:
                    a_round(i)
                low_e(c, E_LOOPS, 0)

            def low_w(c, i, b, ks):
                for k in ks:
                    dve.wait_ge(w_high_ready, 2 * W_UNITS * c + 8 * i + 4 * b + k + 1)
                    nc.vector.tensor_tensor(w_low[:, k, :], raw[:, 2 * b + k // 2, k % 2 * NCOL:(k % 2 + 1) * NCOL],
                                            w_high[:, k, :].bitcast(F32), ALU.subtract).then_inc(w_low_ready, 1)

            def mix(c, tables):
                dve.wait_ge(e_used, HI * (c + 1))
                for k in range(KT):
                    nc.vector.scalar_tensor_tensor(pooled[:, k, :], acc[:, k, 0:CHUNK], unscale_f,
                                                   recip[:, :], ALU.mult, ALU.mult).then_inc(pooled_ready, 1)
                if tables:
                    make_onehots(c + 1, 2, 0)
                    make_onehots(c + 1, 3, 1)
                low_w(c, 0, 0, range(KT))
                for o in range(KT):
                    if tables:
                        make_onehots(c + 1, o + 4, o % 2)
                    dve.wait_ge(gate_ready, KT * c + o + 1)
                    then(nc.vector.tensor_tensor(pooled[:, o, :], user[:, o, :], retrieved[:, o, :], ALU.subtract))
                    then(nc.vector.tensor_tensor(pooled[:, o, :], pooled[:, o, :], gate[:, o, :], ALU.mult))
                    then(nc.vector.tensor_tensor(pooled[:, o, :], pooled[:, o, :], retrieved[:, o, :], ALU.add))
                    then(nc.vector.tensor_copy(mix_high[:, o, :], pooled[:, o, :]))
                    nc.vector.tensor_tensor(mix_low[:, o, :], pooled[:, o, :], mix_high[:, o, :].bitcast(F32),
                                            ALU.subtract).then_inc(mix_ready, 1)

            def take_logits(c, i, b, wait_stored=True):
                dve.wait_ge(w_used, 2 * W_UNITS * c + 4 * (2 * i + b + 1))
                dve.wait_ge(bias_loaded[b], 16 * ((EVEN, ODD)[b] * c + i + 1))
                if wait_stored:
                    dve.wait_ge(stored[b], 16 * ((EVEN, ODD)[b] * c + i))
                nc.vector.tensor_tensor(stage[:, b, :, :], acc[:, 2 * b:2 * b + 2, 0:NCOL],
                                        bias[:, b, :].unsqueeze(1).broadcast_to([P, BT, NCOL]), ALU.add)\
                    .then_inc(logits_taken, 1)

            def logits(c, tables, after):
                def block_of(i, b, split=True):
                    for half in range(2):
                        if split:
                            low_w(c, i, b, (2 * half, 2 * half + 1))
                        if tables:
                            make_onehots(c + 1, 2 * i + b + EARLY, b, (2 * half, 2 * half + 1))

                block_of(0, 0, False)
                block_of(0, 1)
                take_logits(c, 0, 0, False)
                block_of(1, 0)
                take_logits(c, 0, 1, False)
                block_of(1, 1)
                take_logits(c, 1, 0)
                with dve.Fori(2, PAIRS) as i:
                    block_of(i, 0)
                    take_logits(c, i - 1, 1)
                    block_of(i, 1)
                    take_logits(c, i, 0)
                low_w(c, PAIRS, 0, range(KT))
                take_logits(c, PAIRS - 1, 1)
                after()
                take_logits(c, PAIRS, 0)

            def turn(c, more):
                mix(c - 1, True)
                logits(c - 1, True, lambda: (low_e(c, 0, 0), low_e(c, 0, 1)))
                sums(c, more, True)

            dve.wait_ge(ramps_ready, 1)
            then(nc.vector.tensor_scalar(is_hist[:, :], row[:, :], float(SEQ_B), None, ALU.is_lt))
            then(nc.vector.tensor_scalar(is_retr[:, :], is_hist[:, :], -1.0, 1.0, ALU.mult, ALU.add))
            then(nc.vector.tensor_scalar(wrap[:, :], is_retr[:, :], float(ITEMS), None, ALU.mult))
            then(nc.vector.tensor_scalar(hi_off[:, :], is_retr[:, :], float(HI), None, ALU.mult))
            split_a(0)
            split_b()
            dve.wait_ge(ramps_ready, 3)
            make_onehots(0, 0, 0, free=False)
            make_onehots(0, 1, 1, free=False)
            with dve.Fori(1, GROUPS // 2) as i:
                for j in range(2):
                    make_onehots(0, 2 * i + j, j)
            dve.wait_ge(scanned, E_UNITS)
            nc.vector.tensor_reduce(abs_own[:, :], abs_sums[:, :], AX.X, ALU.max).then_inc(abs_own_ready, 1)
            dve.wait_ge(abs_all_ready, 1)
            then(nc.vector.tensor_scalar(exps[:, 0:1], abs_all[:, :].bitcast(I32), 23, None,
                                         ALU.logical_shift_right))
            then(nc.vector.tensor_scalar(exps[:, 1:2], exps[:, 0:1], -1.0, 268.0, ALU.mult, ALU.add))
            then(nc.vector.tensor_scalar(exps[:, 0:1], exps[:, 1:2], 1.0, 253.0, ALU.max, ALU.min))
            then(nc.vector.tensor_scalar(exps[:, 2:3], exps[:, 0:1], -1.0, 254.0, ALU.mult, ALU.add))
            then(nc.vector.tensor_scalar(scale[:, :], exps[:, 0:1], 23, None, ALU.logical_shift_left))
            then(nc.vector.tensor_scalar(unscale[:, :], exps[:, 2:3], 23, None, ALU.logical_shift_left))
            nc.vector.tensor_scalar(retr_scale[:, :], unscale_f, 1.0 / TOPK, None, ALU.mult)\
                .then_inc(scale_ready, 1)
            sums(0, True, False)
            start = taken[0]
            with dve.Fori(1, CHUNKS - 1) as c:
                base[0], taken[0] = start + STEPS * (c - 1), 0
                turn(c, True)
                assert taken[0] == STEPS
            base[0], taken[0] = start + STEPS * (CHUNKS - 2), 0
            turn(CHUNKS - 1, False)
            mix(CHUNKS - 1, False)
            logits(CHUNKS - 1, False, lambda: None)

        @block.tensor
        def _(pe):
            def tables(c, g, slot, wait_taken=True):
                a_lo, a_hi, b_lo, b_hi = onehots(slot)
                pe.wait_ge(onehot_ready, GROUPS * c + g + 1)
                for q in range(2):
                    if wait_taken:
                        pe.wait_ge(table_taken, 2 * (GROUPS * c + g) + q - 1)
                    for j in range(QUAD):
                        u = q * QUAD + j
                        nc.tensor.matmul(table[:, q, j, 0:COLS_B], b_lo[0:ROWS_B, :, u], b_hi[0:ROWS_B, :, u],
                                         start=True, stop=False)
                        last = nc.tensor.matmul(table[:, q, j, 0:HI], a_lo[:, :, u], a_hi[:, :, u],
                                                start=False, stop=True)
                    last.then_inc(table_ready, 1)

            def sum_tile(c, i, j, first=False, final=False):
                tile = 8 * i + j
                pe.wait_ge(e_low_ready, HI * c + tile + 1)
                for k in (2, 3, 0, 1):
                    if first and k == 0 and (not isinstance(c, int) or c > 0):
                        pe.wait_ge(logits_taken, NBLK * c)
                    for part in (e_high, e_low):
                        last = nc.tensor.matmul(
                            acc[:, k, :], part[:, j % 4, k * P:(k + 1) * P],
                            counts[:, bass.ds(tile, 1), :].rearrange("p a b -> p (a b)"),
                            start=first and part is e_high, stop=final and part is e_low)
                last.then_inc(e_used, 1)

            def sums(c):
                pe.wait_ge(table_taken, 2 * GROUPS * (c + 1))
                pe.wait_ge(ids_ready, c + 1)
                nc.tensor.matmul(lengths, ones[:, :], mask[:, 0, :], start=True, stop=False)
                nc.tensor.matmul(lengths, ones[:, :], mask[:, 1, :], start=False, stop=True)\
                    .then_inc(lengths_ready, 1)
                if not isinstance(c, int) or c > 0:
                    pe.wait_ge(logits_taken, NBLK * c - 1)
                for j in range(8):
                    sum_tile(c, 0, j, first=j == 0)
                with pe.Fori(1, E_LOOPS) as i:
                    for j in range(8):
                        sum_tile(c, i, j)
                sum_tile(c, E_LOOPS, 0)
                sum_tile(c, E_LOOPS, 1, final=True)

            def mix(c, with_tables):
                if with_tables:
                    tables(c + 1, 0, 0)
                    tables(c + 1, 1, 1)
                pe.wait_ge(small_loaded, 48)
                pe.wait_ge(pooled_ready, KT * (c + 1))
                pe.wait_ge(retr_ready, KT * (c + 1))
                for o in range(KT):
                    for k in range(KT):
                        last = nc.tensor.matmul(acc[:, o, 0:CHUNK], wrec_sb[:, k, o * P:(o + 1) * P],
                                                pooled[:, k, :], start=k == 0, stop=k == KT - 1)
                    last.then_inc(user_done, 1)
                if with_tables:
                    tables(c + 1, 2, 0)
                pe.wait_ge(gate_loaded, 48 * (c + 1))
                pe.wait_ge(user_ready, KT * (c + 1))
                for o in range(KT):
                    for k in range(2 * KT):
                        weights, rhs = (wgate_retr, retrieved) if k < KT else (wgate_user, user)
                        last = nc.tensor.matmul(acc[:, o, 0:CHUNK], weights[:, k % KT, o * P:(o + 1) * P],
                                                rhs[:, k % KT, :], start=k == 0, stop=k == 2 * KT - 1)
                    last.then_inc(gate_done, 1)
                    if with_tables:
                        tables(c + 1, o + 3, (o + 3) % 2)
                if with_tables:
                    tables(c + 1, 7, 1)

            def logits_block(c, i, b, wait_taken):
                if wait_taken:
                    pe.wait_ge(logits_taken, NBLK * c + 2 * i + b - 1)
                for k in range(KT):
                    pe.wait_ge(w_low_ready, 2 * W_UNITS * c + 8 * i + 4 * b + k + 1)
                    for t in range(BT):
                        to = acc[:, 2 * b + t, 0:NCOL]
                        high, low = (m[:, k, t * P:(t + 1) * P] for m in (mix_high, mix_low))
                        nc.tensor.matmul(to, high, w_high[:, k, :], start=k == 0, stop=False)
                        nc.tensor.matmul(to, high, w_low[:, k, :], start=False, stop=False)
                        last = nc.tensor.matmul(to, low, w_high[:, k, :], start=False, stop=k == KT - 1)
                    last.then_inc(w_used, 1)

            def logits(c, with_tables):
                pe.wait_ge(mix_ready, KT * (c + 1))

                def pair(i, first):
                    for b in range(2):
                        logits_block(c, i, b, not first)
                        if with_tables:
                            tables(c + 1, 2 * i + b + EARLY, b)
                pair(0, True)
                with pe.Fori(1, PAIRS) as i:
                    pair(i, False)
                logits_block(c, PAIRS, 0, True)

            def turn(c):
                mix(c - 1, True)
                logits(c - 1, True)
                sums(c)

            pe.wait_ge(ramps_ready, 3)
            tables(0, 0, 0, False)
            tables(0, 1, 1)
            with pe.Fori(1, GROUPS // 2) as i:
                tables(0, 2 * i, 0)
                tables(0, 2 * i + 1, 1)
            sums(0)
            with pe.Fori(1, CHUNKS - 1) as c:
                turn(c)
            turn(CHUNKS - 1)
            mix(CHUNKS - 1, False)
            logits(CHUNKS - 1, False)


def kernel(**inputs):
    import numpy as np
    import concourse.bacc as bacc
    from concourse.bass_utils import run_bass_kernel_spmd

    x = {k: np.asarray(v) for k, v in inputs.items()}
    seq, retr = x["r_sequence_ids"], x["r_retrieved_indices"]
    ids_a = np.ascontiguousarray(seq[:, :P].T)
    ids_b = np.zeros((P, BATCH), seq.dtype)
    ids_b[:SEQ_B] = seq[:, P:].T
    ids_b[SEQ_B:ROWS_B] = retr.T
    emb = x["L0_rec_item_embeddings"]
    emb_p = np.zeros((HI * P, HID), emb.dtype)
    emb_p[:ITEMS] = emb
    emb_p = np.ascontiguousarray(emb_p.reshape(E_UNITS, 2, P, HID).transpose(0, 2, 1, 3)).reshape(E_UNITS, P, 2 * HID)
    w_rec = np.ascontiguousarray(x["L0_rec_W_rec"].T.reshape(KT, P, HID).transpose(1, 0, 2))
    w_gate = np.ascontiguousarray(x["L0_rec_gate_W"].T.reshape(2 * KT, P, HID).transpose(1, 0, 2))
    w_proj = x["L0_rec_proj_W"].T.reshape(2, 2, P, NBLK, NCOL).transpose(3, 0, 2, 1, 4)
    w_proj = np.ascontiguousarray(w_proj).reshape(W_UNITS, P, 2 * NCOL)
    arrays = {
        "ids_a": ids_a, "ids_b": ids_b, "emb": emb_p, "w_rec": w_rec,
        "b_rec": np.ascontiguousarray(x["L0_rec_b_rec"].reshape(KT, P).T), "w_gate": w_gate,
        "b_gate": np.ascontiguousarray(x["L0_rec_gate_b"].reshape(KT, P).T), "w_proj": w_proj,
        "b_proj": np.ascontiguousarray(x["L0_rec_proj_b"].reshape(NBLK, NCOL)),
    }
    nc = bacc.Bacc("TRN2", target_bir_lowering=False, num_devices=1)
    args = [nc.dram_tensor(n, a.shape, mybir.dt.from_np(a.dtype), kind="ExternalInput").ap() for n, a in arrays.items()]
    out = nc.dram_tensor("logits", (BATCH, ITEMS), F32, kind="ExternalOutput").ap()
    build(nc, *args, out)
    r = run_bass_kernel_spmd(nc, [arrays], core_ids=[0])
    return r.results[0]["logits"]
```

```python
from contextlib import ExitStack

import concourse.bass as bass
from concourse import mybir

ACT = mybir.ActivationFunctionType
ALU = mybir.AluOpType
F32 = mybir.dt.float32
F32R = mybir.dt.float32r
F16 = mybir.dt.float16
BF16 = mybir.dt.bfloat16
I32 = mybir.dt.int32

P = 128
BATCH, SEQ, TOPK, ITEMS, HID = 1024, 200, 50, 12500, 512
KT = HID // P
HI = -(-ITEMS // P)
SEQ_B = SEQ - P
ROWS_B = SEQ_B + TOPK
COLS_B = 2 * HI
VALID = P
CHUNK = 256
CHUNKS = BATCH // CHUNK
BT = CHUNK // P
G = 8
GROUPS = CHUNK // G
QUAD = G // 2
E_UNITS = HI // 2
E_LOOPS, E_REST = divmod(E_UNITS, 4)
NCOL = 500
NBLK = ITEMS // NCOL
W_UNITS = 2 * NBLK
PAIRS = NBLK // 2
EARLY = GROUPS - 2 * PAIRS
assert E_REST == 1 and NBLK == 2 * PAIRS + 1 and HI % 2 == 0 and ROWS_B <= P

RAW = 4
E_PER = [sum((u + 2) % RAW == s for u in range(E_UNITS)) for s in range(RAW)]
W_PER = [sum(w % RAW == s for w in range(W_UNITS)) for s in range(RAW)]
EVEN, ODD = PAIRS + 1, PAIRS


def e_loads(c, slot, i):
    return (E_PER[slot] + W_PER[slot]) * c + i + 1


def w_loads(c, slot, i):
    return (E_PER[slot] + W_PER[slot]) * c + E_PER[slot] + i + 1


EXPONENT, LEAST, RAISED, INVERSE = 255 << 23, 15 << 23, 14 << 23, 254 << 23
STEPS = 3 * KT + 1 + 2 + 6


def build(nc, ids_a, ids_b, emb, w_rec, b_rec, w_gate, b_gate, w_proj, b_proj, out):
    out_v = out.rearrange("(c b p) n -> c p b n", b=BT, p=P)
    with ExitStack() as ctx:
        def sb(name, shape, dt):
            return ctx.enter_context(nc.sbuf_tensor(name, shape, dt))

        def sem(name):
            return ctx.enter_context(nc.semaphore(name))

        counts = sb("counts", [P, HI, 2 * CHUNK], BF16)
        raw = sb("raw", [P, RAW, 2 * HID], F32)
        e_high = sb("e_high", [P, 4, HID], F16)
        e_low = sb("e_low", [P, 4, HID], F16)
        w_high = sb("w_high", [P, 4, NCOL], F32R)
        w_low = sb("w_low", [P, 4, NCOL], F32R)
        onehot = sb("onehot", [P, 2, (2 * P + 3 * HI) * G], BF16)
        ramp = sb("ramp", [P, VALID + HI, G], BF16)
        stage_mem = sb("stage_mem", [P, KT * HID], F32)
        bias_mem = sb("bias_mem", [P, KT * CHUNK], F32)
        wrec_sb = sb("wrec_sb", [P, KT, HID], F32)
        wgate_user = sb("wgate_user", [P, KT, HID], F32)
        user = sb("user", [P, KT, CHUNK], F32)
        mix_high = sb("mix_high", [P, KT, CHUNK], F32R)
        mix_low = sb("mix_low", [P, KT, CHUNK], F32R)
        raw_ids = sb("raw_ids", [P, 2, CHUNK], I32)
        ids = sb("ids", [P, 5, CHUNK], BF16)
        mask = sb("mask", [P, 2, CHUNK], BF16)
        recip = sb("recip", [P, CHUNK], F32)
        ones = sb("ones", [P, P], BF16)
        brec_sb = sb("brec_sb", [P, KT], F32)
        bgate_sb = sb("bgate_sb", [P, KT], F32)
        row = sb("row", [P, 1], I32)
        is_hist = sb("is_hist", [P, 1], F32)
        wrap = sb("wrap", [P, 1], F32)
        retr_valid = sb("retr_valid", [P, 1], F32)
        abs_sums = sb("abs_sums", [P, HI], F32)
        sigmoid_out = sb("sigmoid_out", [P, 1], F32)
        exponent = sb("exponent", [P, 2], I32)
        unscale = sb("unscale", [P, HI], I32)
        scale = sb("scale", [P, HI], I32)
        scale_f, unscale_f = scale[:, :].bitcast(F32), unscale[:, :].bitcast(F32)

        def flat(t):
            return t[:, :, :].rearrange("p a b -> p (a b)")

        def by_tile(view):
            return view.rearrange("p (k b) -> p k b", k=KT)

        pooled = by_tile(flat(e_high).bitcast(F32))
        gate = by_tile(flat(e_low).bitcast(F32))
        stage = stage_mem[:, 0:2 * BT * NCOL].rearrange("p (s b n) -> p s b n", s=2, b=BT)
        wgate_retr = stage_mem[:, :].rearrange("p (k n) -> p k n", k=KT)
        bias = bias_mem[:, 0:2 * NCOL].rearrange("p (s n) -> p s n", s=2)
        retrieved = by_tile(bias_mem[:, :])
        abs_out = bias_mem[:, 0:HID].bitcast(BF16).rearrange("p (t n) -> p t n", t=2)
        place, item = user[:, 0:2, :], user[:, 2:4, :].bitcast(I32)

        acc = ctx.enter_context(nc.psum_tensor("acc", [P, 4, 512], F32))
        table = ctx.enter_context(nc.psum_tensor("table", [P, 2, QUAD, 256], F32))
        lengths = table[:, 0, 0, 0:CHUNK]

        def onehots(slot):
            lo = onehot[:, slot, 0:2 * P * G].rearrange("p (f v g) -> p f v g", f=2, g=G)
            hi = onehot[:, slot, 2 * P * G:].rearrange("p (f v g) -> p f v g", f=3, g=G)
            return lo, hi

        ids_loaded = sem("ids_loaded")
        small_loaded = sem("small_loaded")
        raw_loaded = [sem(f"raw_loaded{s}") for s in range(RAW)]
        gate_loaded = sem("gate_loaded")
        bias_loaded = [sem(f"bias_loaded{s}") for s in range(2)]
        stored = [sem(f"stored{s}") for s in range(2)]
        ramps_ready = sem("ramps_ready")
        dve_step = sem("dve_step")
        ids_ready = sem("ids_ready")
        lengths_ready = sem("lengths_ready")
        abs_ready = sem("abs_ready")
        scale_ready = sem("scale_ready")
        onehot_ready = sem("onehot_ready")
        table_ready = sem("table_ready")
        table_taken = sem("table_taken")
        e_high_ready = sem("e_high_ready")
        e_low_ready = sem("e_low_ready")
        e_used = sem("e_used")
        pooled_ready = sem("pooled_ready")
        retr_ready = sem("retr_ready")
        user_done = sem("user_done")
        user_ready = sem("user_ready")
        gate_done = sem("gate_done")
        gate_ready = sem("gate_ready")
        mix_ready = sem("mix_ready")
        w_high_ready = sem("w_high_ready")
        w_low_ready = sem("w_low_ready")
        w_used = sem("w_used")
        logits_taken = sem("logits_taken")

        block = ctx.enter_context(nc.Block())

        @block.sync
        def _(sp):
            def load_ids(c):
                if not isinstance(c, int) or c > 0:
                    sp.wait_ge(ids_ready, c)
                for n, src in enumerate((ids_a, ids_b)):
                    sp.dma_start(raw_ids[:, n, :], src[:, bass.ds(c * CHUNK, CHUNK)]).then_inc(ids_loaded, 16)

            def load_e(u, slot):
                sp.dma_start(raw[:, slot, :], emb[bass.ds(u, 1)].rearrange("a p n -> p (a n)"))\
                    .then_inc(raw_loaded[slot], 16)

            def load_w(w, slot):
                sp.dma_start(raw[:, slot, 0:2 * NCOL], w_proj[bass.ds(w, 1)].rearrange("a p n -> p (a n)"))\
                    .then_inc(raw_loaded[slot], 16)

            def load_bias(n, slot):
                sp.dma_start(bias[:, slot, :], b_proj[bass.ds(n, 1), :].broadcast_to([P, NCOL]))\
                    .then_inc(bias_loaded[slot], 16)

            def store(c, n, slot):
                sp.wait_ge(logits_taken, NBLK * c + n + 1)
                sp.dma_start(out_v[c, :, :, bass.ds(n * NCOL, NCOL)], stage[:, slot, :, :])\
                    .then_inc(stored[slot], 16)

            def first_embeddings(c):
                for j in range(RAW):
                    if not isinstance(c, int) or c > 0:
                        sp.wait_ge(w_low_ready, 2 * W_UNITS * (c - 1) + 2 * (W_UNITS - 3 + j))
                    load_e(j, (j + 2) % RAW)

            def other_embeddings(c):
                with sp.Fori(1, E_LOOPS) as i:
                    for j in range(RAW):
                        sp.wait_ge(e_low_ready, HI * c + 2 * (4 * i + j - 3))
                        load_e(4 * i + j, (j + 2) % RAW)
                sp.wait_ge(e_low_ready, HI * c + 2 * (E_UNITS - 4))
                load_e(E_UNITS - 1, (E_UNITS + 1) % RAW)

            def load_gate(c):
                again = not isinstance(c, int) or c > 0
                if again:
                    sp.wait_ge(gate_done, KT * c)
                sp.dma_start(wgate_user[:, 0:2, :], w_gate[:, 0:2, :]).then_inc(gate_loaded, 16)
                if again:
                    sp.wait_ge(stored[0], 16 * EVEN * c)
                sp.dma_start(wgate_user[:, 2:4, :], w_gate[:, 2:4, :]).then_inc(gate_loaded, 16)
                if again:
                    sp.wait_ge(stored[1], 16 * ODD * c)
                sp.dma_start(wgate_retr, w_gate[:, KT:2 * KT, :]).then_inc(gate_loaded, 16)

            def first_projection(c):
                for j in range(RAW):
                    sp.wait_ge(e_low_ready, HI * c + min(2 * (E_UNITS - 2 + j), HI))
                    load_w(j, j)

            def logits(c):
                def load_block(i, b):
                    for h in range(2):
                        sp.wait_ge(w_low_ready, 2 * W_UNITS * c + 2 * (4 * i + 2 * b + h - 3))
                        load_w(4 * i + 2 * b + h, 2 * b + h)

                load_block(1, 0)
                sp.wait_ge(mix_ready, KT * (c + 1))
                load_bias(0, 0)
                load_bias(1, 1)
                with sp.Fori(1, PAIRS) as i:
                    for b in range(2):
                        load_block(i + b, 1 - b)
                        store(c, 2 * i - 2 + b, b)
                        load_bias(2 * i + b, b)
                store(c, NBLK - 3, 0)
                load_bias(NBLK - 1, 0)

            def last_stores(c):
                store(c, NBLK - 2, 1)
                store(c, NBLK - 1, 0)

            def turn(c, more):
                logits(c - 1)
                first_embeddings(c)
                last_stores(c - 1)
                if more:
                    load_ids(c + 1)
                other_embeddings(c)
                load_gate(c)
                first_projection(c)

            load_ids(0)
            first_embeddings(0)
            sp.dma_start(wrec_sb[:, :, :], w_rec).then_inc(small_loaded, 16)
            sp.dma_start(brec_sb[:, :], b_rec).then_inc(small_loaded, 16)
            sp.dma_start(bgate_sb[:, :], b_gate).then_inc(small_loaded, 16)
            load_ids(1)
            other_embeddings(0)
            load_gate(0)
            first_projection(0)
            with sp.Fori(1, CHUNKS - 1) as c:
                turn(c, True)
            turn(CHUNKS - 1, False)
            logits(CHUNKS - 1)
            last_stores(CHUNKS - 1)
            sp.wait_ge(stored[0], 16 * EVEN * CHUNKS)
            sp.wait_ge(stored[1], 16 * ODD * CHUNKS)

        @block.gpsimd
        def _(pool):
            nc.gpsimd.iota(row[:, :], pattern=[[0, 1]], base=0, channel_multiplier=1).then_inc(ramps_ready, 1)
            nc.gpsimd.iota(ramp[:, :, :], pattern=[[1, VALID + HI], [0, G]], base=0, channel_multiplier=0,
                           allow_small_or_imprecise_dtypes=True).then_inc(ramps_ready, 1)
            nc.gpsimd.memset(ones[:, :], 1.0).then_inc(ramps_ready, 1)

        @block.scalar
        def _(act):
            def abs_unit(i, j):
                slot = (j + 2) % RAW
                act.wait_ge(raw_loaded[slot], 16 * e_loads(0, slot, i + j // 4))
                for t in range(2):
                    tile = 8 * i + 2 * j + t
                    if not isinstance(tile, int) or tile >= 2:
                        act.wait_ge(abs_ready, tile - 1)
                    nc.scalar.activation(abs_out[:, t, :], raw[:, slot, t * HID:(t + 1) * HID], ACT.Abs,
                                         accum_out=abs_sums[:, bass.ds(tile, 1)]).then_inc(abs_ready, 1)

            def take_tables(c, g):
                for q in range(2):
                    act.wait_ge(table_ready, 2 * (GROUPS * c + g) + q + 1)
                    to = counts[:, :, :].rearrange("p h (w b) -> p w h b", w=2)
                    nc.scalar.activation(
                        to[:, :, :, bass.ds(g * G + q * QUAD, QUAD)],
                        table[:, q, :, 0:COLS_B].rearrange("p b (w h) -> p w h b", w=2),
                        ACT.Copy).then_inc(table_taken, 1)

            def high_e(c, i, j, wait_used):
                slot = (j + 2) % RAW
                act.wait_ge(raw_loaded[slot], 16 * e_loads(c, slot, i))
                for t in range(2):
                    tile = 8 * i + 2 * j + t
                    if wait_used or j >= 2:
                        act.wait_ge(e_used, HI * c + tile - 3)
                    nc.scalar.activation(e_high[:, (2 * j + t) % 4, :], raw[:, slot, t * HID:(t + 1) * HID],
                                         ACT.Copy, scale=scale_f[:, bass.ds(tile, 1)]).then_inc(e_high_ready, 1)

            def sums(c, first):
                def unit(i, j, wait_used=True):
                    if first:
                        abs_unit(i, j + 1)
                        act.wait_ge(scale_ready, 4 * i + j + 1)
                    high_e(c, i, j, wait_used)

                for j in range(1 if first else 0, 4):
                    unit(0, j, False)
                with act.Fori(1, E_LOOPS) as i:
                    for j in range(4):
                        unit(i, j)
                if first:
                    act.wait_ge(scale_ready, E_UNITS)
                high_e(c, E_LOOPS, 0, True)

            def high_w(c, i, b, wait_used):
                for k in range(KT):
                    slot = 2 * b + k // 2
                    if k % 2 == 0:
                        act.wait_ge(raw_loaded[slot], 16 * w_loads(c, slot, i))
                    if wait_used:
                        act.wait_ge(w_used, 2 * W_UNITS * c + 8 * i + 4 * b + k - 3)
                    nc.scalar.activation(w_high[:, k, :], raw[:, slot, k % 2 * NCOL:(k % 2 + 1) * NCOL],
                                         ACT.Copy).then_inc(w_high_ready, 1)

            def mix(c, tables):
                act.wait_ge(e_used, HI * (c + 1))
                for k in range(KT):
                    act.wait_ge(pooled_ready, KT * c + k + 1)
                    nc.scalar.activation(retrieved[:, k, :], acc[:, k, CHUNK:2 * CHUNK], ACT.Copy,
                                         scale=1.0 / TOPK).then_inc(retr_ready, 1)
                if tables:
                    take_tables(c + 1, 0)
                    take_tables(c + 1, 1)
                act.wait_ge(small_loaded, 48)
                for o in range(KT):
                    act.wait_ge(user_done, KT * c + o + 1)
                    nc.scalar.activation(user[:, o, :], acc[:, o, 0:CHUNK], ACT.Identity,
                                         bias=brec_sb[:, o:o + 1]).then_inc(user_ready, 1)
                if tables:
                    take_tables(c + 1, 2)
                high_w(c, 0, 0, False)
                for o in range(KT):
                    act.wait_ge(gate_done, KT * c + o + 1)
                    nc.scalar.activation(gate[:, o, :], acc[:, o, 0:CHUNK], ACT.Sigmoid,
                                         bias=bgate_sb[:, o:o + 1]).then_inc(gate_ready, 1)
                    if tables:
                        take_tables(c + 1, o + 3)

            def logits(c, tables):
                def block_of(i, b):
                    high_w(c, i, b, True)
                    if tables:
                        take_tables(c + 1, 2 * i + b + EARLY - 1)
                high_w(c, 0, 1, True)
                if tables:
                    take_tables(c + 1, EARLY - 1)
                    take_tables(c + 1, EARLY)
                with act.Fori(1, PAIRS) as i:
                    block_of(i, 0)
                    block_of(i, 1)
                high_w(c, PAIRS, 0, True)
                if tables:
                    take_tables(c + 1, GROUPS - 1)

            def turn(c):
                mix(c - 1, True)
                logits(c - 1, True)
                act.wait_ge(mix_ready, KT * c)
                sums(c, False)

            act.wait_ge(ramps_ready, 3)
            nc.scalar.activation(sigmoid_out[:, :], ones[:, 0:1], ACT.Sigmoid)
            abs_unit(0, 0)
            abs_unit(0, 1)
            with act.Fori(0, GROUPS // 2 - 1) as i:
                take_tables(0, 2 * i)
                take_tables(0, 2 * i + 1)
            act.wait_ge(scale_ready, 1)
            high_e(0, 0, 0, False)
            take_tables(0, GROUPS - 2)
            take_tables(0, GROUPS - 1)
            sums(0, True)
            with act.Fori(1, CHUNKS - 1) as c:
                turn(c)
            turn(CHUNKS - 1)
            mix(CHUNKS - 1, False)
            logits(CHUNKS - 1, False)

        @block.vector
        def _(dve):
            base, taken = [0], [0]

            def then(ins):
                taken[0] += 1
                ins.then_inc(dve_step, 1)
                dve.wait_ge(dve_step, base[0] + taken[0])

            def clamp_ids(c):
                dve.wait_ge(ids_loaded, 32 * (c + 1))
                then(nc.vector.tensor_scalar(place[:, 1, :], raw_ids[:, 1, :], 0.0, wrap[:, :], ALU.is_lt, ALU.mult))
                nc.vector.tensor_scalar(place[:, 0, :], raw_ids[:, 0, :], -1.0, None, ALU.add)
                then(nc.vector.scalar_tensor_tensor(place[:, 1, :], raw_ids[:, 1, :], is_hist[:, :],
                                                    place[:, 1, :], ALU.subtract, ALU.add))
                then(nc.vector.tensor_scalar(item, place, 0.0, float(ITEMS - 1), ALU.max, ALU.min))
                nc.vector.tensor_scalar(mask[:, 0, :], raw_ids[:, 0, :], 0.0, None, ALU.not_equal)
                then(nc.vector.tensor_scalar(mask[:, 1, :], raw_ids[:, 1, :], 0.0, is_hist[:, :],
                                             ALU.not_equal, ALU.mult))

            def split_items(c):
                hi_part, lo_part = place.bitcast(I32), item
                then(nc.vector.tensor_scalar(hi_part, item, 7, None, ALU.logical_shift_right))
                then(nc.vector.tensor_scalar(lo_part, item, P - 1, None, ALU.bitwise_and))
                nc.vector.tensor_copy(ids[:, 0:2, :], lo_part)
                nc.vector.scalar_tensor_tensor(ids[:, 2:4, :], mask[:, :, :], float(VALID), hi_part,
                                               ALU.mult, ALU.add)
                nc.vector.tensor_scalar(ids[:, 4, :], hi_part[:, 1, :], retr_valid[:, :], None, ALU.add)\
                    .then_inc(ids_ready, 1)
                dve.wait_ge(ids_ready, c + 1)

            def make_onehots(c, g, slot, parts=(0, 1), free=True):
                if free and 0 in parts:
                    dve.wait_ge(table_ready, 2 * (GROUPS * c + g) - 2)
                for n in parts:
                    view = onehots(slot)[n]
                    values = (ramp[:, 0:P, :], ramp[:, VALID:VALID + HI, :])[n]
                    at = ids[:, (0, 2)[n]:(2, 5)[n], bass.ds(g * G, G)]
                    ins = nc.vector.tensor_tensor(view, values.unsqueeze(1).broadcast_to(list(view.shape)),
                                                  at.unsqueeze(2).broadcast_to(list(view.shape)), ALU.is_equal)
                    if n == 1:
                        ins.then_inc(onehot_ready, 1)

            def find_scales(i, j):
                two = bass.ds(8 * i + 2 * j, 2)
                dve.wait_ge(abs_ready, 8 * i + 2 * j + 2)
                then(nc.vector.tensor_scalar(exponent[:, :], abs_sums[:, two].bitcast(I32), EXPONENT, None,
                                             ALU.bitwise_and))
                then(nc.vector.tensor_scalar(unscale[:, two], exponent[:, :], float(LEAST), float(-RAISED),
                                             ALU.max, ALU.add))
                nc.vector.tensor_scalar(scale[:, two], unscale[:, two], -1.0, float(INVERSE), ALU.mult, ALU.add)\
                    .then_inc(scale_ready, 1)

            def low_e(c, i, j):
                slot = (j + 2) % RAW
                for t in range(2):
                    s = (2 * j + t) % 4
                    tile = bass.ds(8 * i + 2 * j + t, 1)
                    nc.vector.tensor_scalar(counts[:, tile, :], counts[:, tile, :], unscale_f[:, tile], None, ALU.mult)
                    dve.wait_ge(e_high_ready, HI * c + 8 * i + 2 * j + t + 1)
                    nc.vector.scalar_tensor_tensor(e_low[:, s, :], raw[:, slot, t * HID:(t + 1) * HID],
                                                   scale_f[:, tile], e_high[:, s, :], ALU.mult, ALU.subtract)\
                        .then_inc(e_low_ready, 1)

            def begin_sums(c, first):
                dve.wait_ge(table_taken, 2 * GROUPS * (c + 1))
                if first:
                    find_scales(0, 1)
                low_e(c, 0, 0)

            def sums(c, more, first):
                def a_round(i, js=range(4)):
                    for j in js:
                        if first:
                            find_scales(i, j + 1)
                        low_e(c, i, j)

                a_round(0, (1, 2, 3))
                dve.wait_ge(lengths_ready, c + 1)
                then(nc.vector.tensor_scalar(recip[:, :], lengths, 1.0, None, ALU.max))
                then(nc.vector.reciprocal(recip[:, :], recip[:, :]))
                if more:
                    a_round(1)
                    clamp_ids(c + 1)
                    a_round(2)
                    split_items(c + 1)
                    a_round(3)
                    make_onehots(c + 1, 0, 0)
                    a_round(4)
                    make_onehots(c + 1, 1, 1)
                steps, done, begin = 8 if first else 0, base[0] + taken[0], 5 if more else 1
                with dve.Fori(begin, E_LOOPS) as i:
                    if first:
                        base[0], taken[0] = done + steps * (i - begin), 0
                    a_round(i)
                if first:
                    base[0], taken[0] = done + steps * (E_LOOPS - begin), 0
                low_e(c, E_LOOPS, 0)

            def low_w(c, i, b, ks):
                for k in ks:
                    dve.wait_ge(w_high_ready, 2 * W_UNITS * c + 8 * i + 4 * b + k + 1)
                    nc.vector.tensor_tensor(w_low[:, k, :], raw[:, 2 * b + k // 2, k % 2 * NCOL:(k % 2 + 1) * NCOL],
                                            w_high[:, k, :].bitcast(F32), ALU.subtract).then_inc(w_low_ready, 1)

            def mix(c, tables):
                dve.wait_ge(e_used, HI * (c + 1))
                for k in range(KT):
                    nc.vector.tensor_tensor(pooled[:, k, :], acc[:, k, 0:CHUNK], recip[:, :], ALU.mult)\
                        .then_inc(pooled_ready, 1)
                if tables:
                    make_onehots(c + 1, 2, 0)
                    make_onehots(c + 1, 3, 1)
                dve.wait_ge(user_ready, KT * (c + 1))
                then(nc.vector.tensor_tensor(pooled, user[:, :, :], retrieved, ALU.subtract))
                low_w(c, 0, 0, range(KT))
                for o in range(KT):
                    dve.wait_ge(gate_ready, KT * c + o + 1)
                    then(nc.vector.tensor_tensor(pooled[:, o, :], pooled[:, o, :], gate[:, o, :], ALU.mult))
                    then(nc.vector.tensor_tensor(pooled[:, o, :], pooled[:, o, :], retrieved[:, o, :], ALU.add))
                    then(nc.vector.tensor_copy(mix_high[:, o, :], pooled[:, o, :]))
                    nc.vector.tensor_tensor(mix_low[:, o, :], pooled[:, o, :], mix_high[:, o, :].bitcast(F32),
                                            ALU.subtract).then_inc(mix_ready, 1)
                    if tables:
                        make_onehots(c + 1, o + 4, o % 2)

            def take_logits(c, i, b, wait_stored=True):
                dve.wait_ge(w_used, 2 * W_UNITS * c + 4 * (2 * i + b + 1))
                dve.wait_ge(bias_loaded[b], 16 * ((EVEN, ODD)[b] * c + i + 1))
                if wait_stored:
                    dve.wait_ge(stored[b], 16 * ((EVEN, ODD)[b] * c + i))
                nc.vector.tensor_tensor(stage[:, b, :, :], acc[:, 2 * b:2 * b + 2, 0:NCOL],
                                        bias[:, b, :].unsqueeze(1).broadcast_to([P, BT, NCOL]), ALU.add)\
                    .then_inc(logits_taken, 1)

            def logits(c, tables, after):
                def block_of(i, b):
                    for half in range(2):
                        low_w(c, i, b, (2 * half, 2 * half + 1))
                        if tables:
                            make_onehots(c + 1, 2 * i + b + EARLY, b, (half,))

                low_w(c, 0, 1, (0, 1))
                if tables:
                    make_onehots(c + 1, EARLY, 0)
                low_w(c, 0, 1, (2, 3))
                if tables:
                    make_onehots(c + 1, EARLY + 1, 1)
                take_logits(c, 0, 0, False)
                block_of(1, 0)
                take_logits(c, 0, 1, False)
                block_of(1, 1)
                take_logits(c, 1, 0)
                with dve.Fori(2, PAIRS) as i:
                    block_of(i, 0)
                    take_logits(c, i - 1, 1)
                    block_of(i, 1)
                    take_logits(c, i, 0)
                low_w(c, PAIRS, 0, range(KT))
                take_logits(c, PAIRS - 1, 1)
                after()
                take_logits(c, PAIRS, 0)

            def turn(c, more):
                mix(c - 1, True)
                logits(c - 1, True, lambda: begin_sums(c, False))
                sums(c, more, False)

            dve.wait_ge(ramps_ready, 1)
            then(nc.vector.tensor_scalar(is_hist[:, :], row[:, :], float(SEQ_B), None, ALU.is_lt))
            then(nc.vector.tensor_scalar(wrap[:, :], is_hist[:, :], float(-ITEMS), float(ITEMS), ALU.mult, ALU.add))
            then(nc.vector.tensor_scalar(retr_valid[:, :], is_hist[:, :], float(-VALID), float(VALID),
                                         ALU.mult, ALU.add))
            clamp_ids(0)
            split_items(0)
            dve.wait_ge(ramps_ready, 3)
            make_onehots(0, 0, 0, free=False)
            make_onehots(0, 1, 1, free=False)
            find_scales(0, 0)
            with dve.Fori(1, GROUPS // 2) as i:
                for j in range(2):
                    make_onehots(0, 2 * i + j, j)
            begin_sums(0, True)
            sums(0, True, True)
            start = base[0] + taken[0]
            with dve.Fori(1, CHUNKS - 1) as c:
                base[0], taken[0] = start + STEPS * (c - 1), 0
                turn(c, True)
                assert taken[0] == STEPS
            base[0], taken[0] = start + STEPS * (CHUNKS - 2), 0
            turn(CHUNKS - 1, False)
            mix(CHUNKS - 1, False)
            logits(CHUNKS - 1, False, lambda: None)

        @block.tensor
        def _(pe):
            def tables(c, g, slot, wait_taken=True):
                lo, hi = onehots(slot)
                hi_of_b = hi[:, 1:3, :, :].rearrange("p f v g -> p (f v) g")
                pe.wait_ge(onehot_ready, GROUPS * c + g + 1)
                for q in range(2):
                    if wait_taken:
                        pe.wait_ge(table_taken, 2 * (GROUPS * c + g) + q - 1)
                    for j in range(QUAD):
                        u = q * QUAD + j
                        nc.tensor.matmul(table[:, q, j, 0:COLS_B], lo[0:ROWS_B, 1, :, u],
                                         hi_of_b[0:ROWS_B, :, u],
                                         start=True, stop=False)
                        last = nc.tensor.matmul(table[:, q, j, 0:HI], lo[:, 0, :, u], hi[:, 0, :, u],
                                                start=False, stop=True)
                    last.then_inc(table_ready, 1)

            def sum_tile(c, i, j, first=False, final=False):
                tile = 8 * i + j
                pe.wait_ge(e_low_ready, HI * c + tile + 1)
                for k in (2, 3, 0, 1):
                    if first and k == 0 and (not isinstance(c, int) or c > 0):
                        pe.wait_ge(logits_taken, NBLK * c)
                    for part in (e_high, e_low):
                        last = nc.tensor.matmul(
                            acc[:, k, :], part[:, j % 4, k * P:(k + 1) * P],
                            counts[:, bass.ds(tile, 1), :].rearrange("p a b -> p (a b)"),
                            start=first and part is e_high, stop=final and part is e_low)
                last.then_inc(e_used, 1)

            def sums(c):
                pe.wait_ge(table_taken, 2 * GROUPS * (c + 1))
                pe.wait_ge(ids_ready, c + 1)
                nc.tensor.matmul(lengths, ones[:, :], mask[:, 0, :], start=True, stop=False)
                nc.tensor.matmul(lengths, ones[:, :], mask[:, 1, :], start=False, stop=True)\
                    .then_inc(lengths_ready, 1)
                if not isinstance(c, int) or c > 0:
                    pe.wait_ge(logits_taken, NBLK * c - 1)
                for j in range(8):
                    sum_tile(c, 0, j, first=j == 0)
                with pe.Fori(1, E_LOOPS) as i:
                    for j in range(8):
                        sum_tile(c, i, j)
                sum_tile(c, E_LOOPS, 0)
                sum_tile(c, E_LOOPS, 1, final=True)

            def mix(c, with_tables):
                if with_tables:
                    tables(c + 1, 0, 0)
                pe.wait_ge(small_loaded, 48)

                def to_user(o, k):
                    return nc.tensor.matmul(acc[:, o, 0:CHUNK], wrec_sb[:, k, o * P:(o + 1) * P],
                                            pooled[:, k, :], start=k == 0, stop=k == KT - 1)

                for k in range(2):
                    pe.wait_ge(pooled_ready, KT * c + k + 1)
                    for o in range(KT):
                        if k == 0:
                            pe.wait_ge(retr_ready, KT * c + o + 1)
                        to_user(o, k)
                if with_tables:
                    tables(c + 1, 1, 1)
                for o in range(KT):
                    for k in range(2, KT):
                        if o == 0:
                            pe.wait_ge(pooled_ready, KT * c + k + 1)
                        last = to_user(o, k)
                    last.then_inc(user_done, 1)
                if with_tables:
                    tables(c + 1, 2, 0)
                pe.wait_ge(gate_loaded, 48 * (c + 1))
                for o in range(KT):
                    pe.wait_ge(user_ready, KT * c + o + 1)
                    for k in range(2 * KT):
                        if o == 0 and k == KT:
                            pe.wait_ge(user_ready, KT * (c + 1))
                        weights, rhs = (wgate_retr, retrieved) if k < KT else (wgate_user, user)
                        last = nc.tensor.matmul(acc[:, o, 0:CHUNK], weights[:, k % KT, o * P:(o + 1) * P],
                                                rhs[:, k % KT, :], start=k == 0, stop=k == 2 * KT - 1)
                    last.then_inc(gate_done, 1)
                    if with_tables:
                        tables(c + 1, o + 3, (o + 3) % 2)

            def logits_block(c, i, b, wait_taken, halfway=lambda: None):
                if wait_taken:
                    pe.wait_ge(logits_taken, NBLK * c + 2 * i + b - 1)
                for k in range(KT):
                    if k == KT // 2:
                        halfway()
                    if not wait_taken:
                        pe.wait_ge(mix_ready, KT * c + max(k + 1, BT * (b + 1)))
                    pe.wait_ge(w_low_ready, 2 * W_UNITS * c + 8 * i + 4 * b + k + 1)
                    for t in range(BT):
                        to = acc[:, 2 * b + t, 0:NCOL]
                        high, low = (m[:, k, t * P:(t + 1) * P] for m in (mix_high, mix_low))
                        nc.tensor.matmul(to, high, w_high[:, k, :], start=k == 0, stop=False)
                        nc.tensor.matmul(to, high, w_low[:, k, :], start=False, stop=False)
                        last = nc.tensor.matmul(to, low, w_high[:, k, :], start=False, stop=k == KT - 1)
                    last.then_inc(w_used, 1)

            def logits(c, with_tables):
                def pair(i, first):
                    for b in range(2):
                        late = with_tables and first
                        if late and b == 1:
                            logits_block(c, i, b, False, lambda: tables(c + 1, EARLY, 0))
                        else:
                            logits_block(c, i, b, not first)
                        if with_tables:
                            tables(c + 1, 2 * i + b + EARLY - (late and b == 0), 1 if late else b)
                pair(0, True)
                with pe.Fori(1, PAIRS) as i:
                    pair(i, False)
                logits_block(c, PAIRS, 0, True)

            def turn(c):
                mix(c - 1, True)
                logits(c - 1, True)
                sums(c)

            pe.wait_ge(ramps_ready, 3)
            tables(0, 0, 0, False)
            tables(0, 1, 1)
            with pe.Fori(1, GROUPS // 2) as i:
                tables(0, 2 * i, 0)
                tables(0, 2 * i + 1, 1)
            sums(0)
            with pe.Fori(1, CHUNKS - 1) as c:
                turn(c)
            turn(CHUNKS - 1)
            mix(CHUNKS - 1, False)
            logits(CHUNKS - 1, False)


def kernel(**inputs):
    import numpy as np
    import concourse.bacc as bacc
    from concourse.bass_utils import run_bass_kernel_spmd

    x = {k: np.asarray(v) for k, v in inputs.items()}
    seq, retr = x["r_sequence_ids"], x["r_retrieved_indices"]
    ids_a = np.ascontiguousarray(seq[:, :P].T)
    ids_b = np.zeros((P, BATCH), seq.dtype)
    ids_b[:SEQ_B] = seq[:, P:].T
    ids_b[SEQ_B:ROWS_B] = retr.T
    emb = x["L0_rec_item_embeddings"]
    emb_p = np.zeros((HI * P, HID), emb.dtype)
    emb_p[:ITEMS] = emb
    emb_p = np.ascontiguousarray(emb_p.reshape(E_UNITS, 2, P, HID).transpose(0, 2, 1, 3)).reshape(E_UNITS, P, 2 * HID)
    w_rec = np.ascontiguousarray(x["L0_rec_W_rec"].T.reshape(KT, P, HID).transpose(1, 0, 2))
    w_gate = np.ascontiguousarray(x["L0_rec_gate_W"].T.reshape(2 * KT, P, HID).transpose(1, 0, 2))
    w_proj = x["L0_rec_proj_W"].T.reshape(2, 2, P, NBLK, NCOL).transpose(3, 0, 2, 1, 4)
    w_proj = np.ascontiguousarray(w_proj).reshape(W_UNITS, P, 2 * NCOL)
    arrays = {
        "ids_a": ids_a, "ids_b": ids_b, "emb": emb_p, "w_rec": w_rec,
        "b_rec": np.ascontiguousarray(x["L0_rec_b_rec"].reshape(KT, P).T), "w_gate": w_gate,
        "b_gate": np.ascontiguousarray(x["L0_rec_gate_b"].reshape(KT, P).T), "w_proj": w_proj,
        "b_proj": np.ascontiguousarray(x["L0_rec_proj_b"].reshape(NBLK, NCOL)),
    }
    nc = bacc.Bacc("TRN2", target_bir_lowering=False, num_devices=1)
    args = [nc.dram_tensor(n, a.shape, mybir.dt.from_np(a.dtype), kind="ExternalInput").ap() for n, a in arrays.items()]
    out = nc.dram_tensor("logits", (BATCH, ITEMS), F32, kind="ExternalOutput").ap()
    build(nc, *args, out)
    r = run_bass_kernel_spmd(nc, [arrays], core_ids=[0])
    return r.results[0]["logits"]
```
